# Optimizing a Trainium2 kernel written in Bass

```python
import numpy as np
import jax
import jax.numpy as jnp

def _softmax(x, axis=-1):
    return jax.nn.softmax(x, axis=axis)

def _gelu(x):
    return jax.nn.gelu(x, approximate=True)

def _silu(x):
    return jax.nn.silu(x)

def _sigmoid(x):
    return jax.nn.sigmoid(x)

def _layernorm(x, axis=-1, eps=1e-05):
    m = jnp.mean(x, axis=axis, keepdims=True)
    v = jnp.var(x, axis=axis, keepdims=True)
    return (x - m) / jnp.sqrt(v + eps)

def _scatter_add(tgt, idx, src, axis=0):
    return tgt.at[idx].add(src)

def _segment_sum(src, seg, n):
    return jax.ops.segment_sum(src, seg, n)
kernel_name = 'mk_flamingo_gated_d1_seqx_r4_5b48bb'

def setup_inputs(seed: int=0):
    np.random.seed(seed)
    _w = jnp.asarray

    def _rec_inputs():
        import jax
        import jax.numpy as jnp
        _rk = jax.random.key(seed)
        x = -0.000125 + 0.9999 * jax.random.normal(jax.random.fold_in(_rk, 1), (4, 512, 512), jnp.float32)
        _lenS = 512 - jax.random.randint(jax.random.fold_in(_rk, 7), (4,), 0, max(1, 512 // 4) + 1, jnp.int32)
        _lenS2 = 512 - jax.random.randint(jax.random.fold_in(_rk, 8), (4,), 0, max(1, 512 // 4) + 1, jnp.int32)
        fside_BxS2xS2_0 = -3.05549e-07 + 0.0199987 * jax.random.normal(jax.random.fold_in(_rk, 11), (4, 512, 512), jnp.float32)
        _ctx_1024P = jax.random.normal(jax.random.fold_in(_rk, 12), (4, 16, 256), jnp.float32)
        _ctx_1024c = jax.random.dirichlet(jax.random.fold_in(_rk, 512), 0.3 * jnp.ones((16,), jnp.float32), (4, 512))
        _ctx_1024t = jnp.einsum('bsk,bkd->bsd', _ctx_1024c, _ctx_1024P)
        _ctx_1024t = _ctx_1024t * jax.lax.rsqrt(jnp.mean(jnp.square(_ctx_1024t)) + 1e-12) * 0.953939
        ctx_1024 = 6.82029e-06 + 0.0200006 * (_ctx_1024t + 0.3 * jax.random.normal(jax.random.fold_in(_rk, 612), (4, 512, 256), jnp.float32))
        _g = jax.random.normal(jax.random.fold_in(_rk, 9001), (2, 1), jnp.float32)
        _g = jnp.sign(_g) * jnp.maximum(jnp.abs(_g), 1.0) + (_g == 0) * 1.0
        g_xattn = _g[0]
        g_ffn = _g[1]
        return (x, fside_BxS2xS2_0, ctx_1024, g_xattn, g_ffn)
    x, fside_BxS2xS2_0, ctx_1024, g_xattn, g_ffn = _rec_inputs()

    def _L0_xattn_setup():
        import jax, jax.numpy as jnp
        import numpy as np
        EPS = 1e-06
        QMAX = 127.0

        def _smooth_quant_linear(x, w):
            amax_x = jnp.max(jnp.abs(x), axis=0)
            amax_w = jnp.max(jnp.abs(w), axis=0)
            s = jnp.sqrt(jnp.maximum(amax_x, EPS) / jnp.maximum(amax_w, EPS))
            s = jnp.maximum(s, EPS)
            xs = x / s
            ws = w * s
            x_scale = jnp.maximum(jnp.max(jnp.abs(xs), axis=-1, keepdims=True), EPS) / QMAX
            w_scale = jnp.maximum(jnp.max(jnp.abs(ws), axis=-1, keepdims=True), EPS) / QMAX
            x_q = jnp.clip(jnp.round(xs / x_scale), -QMAX, QMAX)
            w_q = jnp.clip(jnp.round(ws / w_scale), -QMAX, QMAX)
            return x_q @ w_q.T * x_scale * w_scale.T

        def _expert_forward(xe, guw, dw):
            h = _smooth_quant_linear(xe, guw)
            gate, up = jnp.split(h, 2, axis=-1)
            a = jax.nn.silu(gate) * up
            return _smooth_quant_linear(a, dw)
        key = jax.random.key(seed)
        k1, k2, k3 = jax.random.split(key, 3)
        E, T, D, I = (8, 512, 512, 256)
        x = jax.random.normal(k1, (E, T, D), dtype=jnp.float32)
        gate_up_weight = jax.random.normal(k2, (E, 2 * I, D), dtype=jnp.float32) * 0.02
        down_weight = jax.random.normal(k3, (E, D, I), dtype=jnp.float32) * 0.02
        return {'x': x, 'gate_up_weight': gate_up_weight, 'down_weight': down_weight}
    _L0_xattn_all = _L0_xattn_setup()
    _L0_xattn_in = {k: v for k, v in _L0_xattn_all.items() if k in ()}
    del _L0_xattn_all

    def _L0_ffn_setup():
        import jax, jax.numpy as jnp
        import numpy as np
        NUM_EXPERTS = 32
        TOP_K = 8
        THRESHOLD = 0.8
        HIDDEN = 512
        INTER = 192
        key = jax.random.key(seed)
        k1, k2, k3, k4 = jax.random.split(key, 4)
        hidden_states = jax.random.normal(k1, (2, 256, HIDDEN), jnp.float32)
        gate_weight = jax.random.normal(k2, (NUM_EXPERTS, HIDDEN), jnp.float32) * 0.02
        gate_up_proj = jax.random.normal(k3, (NUM_EXPERTS, 2 * INTER, HIDDEN), jnp.float32) * 0.02
        down_proj = jax.random.normal(k4, (NUM_EXPERTS, HIDDEN, INTER), jnp.float32) * 0.02
        return {'hidden_states': hidden_states, 'gate_weight': gate_weight, 'gate_up_proj': gate_up_proj, 'down_proj': down_proj}
    _L0_ffn_all = _L0_ffn_setup()
    _L0_ffn_in = {k: v for k, v in _L0_ffn_all.items() if k in ('gate_weight', 'gate_up_proj', 'down_proj')}
    del _L0_ffn_all
    return {'x': x, 'fside_BxS2xS2_0': fside_BxS2xS2_0, 'ctx_1024': ctx_1024, 'g_xattn': g_xattn, 'g_ffn': g_ffn, 'L0_ffn_gate_weight': _L0_ffn_in['gate_weight'], 'L0_ffn_gate_up_proj': _L0_ffn_in['gate_up_proj'], 'L0_ffn_down_proj': _L0_ffn_in['down_proj']}

def reference(x, fside_BxS2xS2_0, ctx_1024, g_xattn, g_ffn, L0_ffn_gate_weight, L0_ffn_gate_up_proj, L0_ffn_down_proj):
    import jax
    import jax.numpy as jnp

    def _L0_xattn_ref(x, gate_up_weight, down_weight):
        import jax, jax.numpy as jnp
        import numpy as np
        EPS = 1e-06
        QMAX = 127.0

        def _smooth_quant_linear(x, w):
            amax_x = jnp.max(jnp.abs(x), axis=0)
            amax_w = jnp.max(jnp.abs(w), axis=0)
            s = jnp.sqrt(jnp.maximum(amax_x, EPS) / jnp.maximum(amax_w, EPS))
            s = jnp.maximum(s, EPS)
            xs = x / s
            ws = w * s
            x_scale = jnp.maximum(jnp.max(jnp.abs(xs), axis=-1, keepdims=True), EPS) / QMAX
            w_scale = jnp.maximum(jnp.max(jnp.abs(ws), axis=-1, keepdims=True), EPS) / QMAX
            x_q = jnp.clip(jnp.round(xs / x_scale), -QMAX, QMAX)
            w_q = jnp.clip(jnp.round(ws / w_scale), -QMAX, QMAX)
            return x_q @ w_q.T * x_scale * w_scale.T

        def _expert_forward(xe, guw, dw):
            h = _smooth_quant_linear(xe, guw)
            gate, up = jnp.split(h, 2, axis=-1)
            a = jax.nn.silu(gate) * up
            return _smooth_quant_linear(a, dw)
        return jax.vmap(_expert_forward)(x, gate_up_weight, down_weight)

    def _L0_ffn_ref(hidden_states, gate_weight, gate_up_proj, down_proj):
        import jax, jax.numpy as jnp
        import numpy as np
        NUM_EXPERTS = 32
        TOP_K = 8
        THRESHOLD = 0.8
        HIDDEN = 512
        INTER = 192
        B, S, H = hidden_states.shape
        x = hidden_states.reshape(-1, H)
        logits = x @ gate_weight.T
        probs = jax.nn.softmax(logits.astype(jnp.float32), axis=-1).astype(logits.dtype)
        top_vals, top_idx = jax.lax.top_k(probs, TOP_K)
        renorm = top_vals / jnp.clip(jnp.sum(top_vals, axis=-1, keepdims=True), 1e-12)
        cum = jnp.cumsum(renorm, axis=-1)
        num_keep = jnp.minimum(jnp.sum((cum < THRESHOLD).astype(jnp.int32), axis=-1) + 1, TOP_K)
        active = jnp.arange(TOP_K)[None, :] < num_keep[:, None]
        rw = top_vals * active.astype(top_vals.dtype)
        rw = rw / jnp.clip(jnp.sum(rw, axis=-1, keepdims=True), 1e-12)
        combine = jnp.sum(jax.nn.one_hot(top_idx, NUM_EXPERTS, dtype=rw.dtype) * rw[..., None], axis=1)

        def body(acc, params):
            w_gu, w_d, ce = params
            gu = x @ w_gu.T
            g, u = jnp.split(gu, 2, axis=-1)
            h = jax.nn.silu(g) * u
            return (acc + h @ w_d.T * ce[:, None], None)
        out, _ = jax.lax.scan(body, jnp.zeros_like(x), (gate_up_proj, down_proj, combine.T))
        return out.reshape(B, S, H)
    x = x + jnp.tanh(g_xattn[0]) * _L0_xattn_ref(_layernorm(x, axis=-1), fside_BxS2xS2_0, ctx_1024)
    x = x + jnp.tanh(g_ffn[0]) * _L0_ffn_ref(_layernorm(x, axis=-1), L0_ffn_gate_weight, L0_ffn_gate_up_proj, L0_ffn_down_proj)
    return x

_drawn_inputs = setup_inputs


def setup_inputs(seed=0):
    import zlib

    import numpy as np

    out = dict(_drawn_inputs(seed))
    spreads = {}
    factors = {'L0_ffn_gate_weight': 5.384, 'L0_ffn_gate_up_proj': 4.75, 'L0_ffn_down_proj': 4.768}
    for name, (base, spread) in spreads.items():
        noise = np.random.default_rng([zlib.crc32(name.encode()), seed]).standard_normal(out[name].shape)
        drawn = base * np.exp(spread * noise) if base else spread * noise
        out[name] = jnp.asarray(drawn.astype(out[name].dtype))
    for name, factor in factors.items():
        out[name] = (out[name] * factor).astype(out[name].dtype)
    return out
```

```python
from contextlib import ExitStack

import concourse.bass as bass
from concourse import mybir

P = 128
STEPS_PER_PASS = 158
ALU = mybir.AluOpType
ACT = mybir.ActivationFunctionType
F32 = mybir.dt.float32
BF16 = mybir.dt.bfloat16
FP16 = mybir.dt.float16
I32 = mybir.dt.int32
U32 = mybir.dt.uint32
AX = mybir.AxisListType

EPS_Q = 1e-6
EPS_LN = 1e-5
QMAX = 127.0
MAGIC = 1.5 * 2.0 ** 23
TOP_K = 8
THRESHOLD = 0.8
SUM_FLOOR = 1e-12


def build(nc, x, w1, w2, g_x, g_f, gate_w, gate_up_t, down_t, out):
    B, T, D = x.shape
    I = w2.shape[2]
    E, _, GU = gate_up_t.shape
    F = GU // 2
    TT = T // P
    DC = D // P
    IC = I // P
    NK = B * TT
    N = B * T
    FREST = F - P
    TILES = N * TOP_K // P + E
    TABW = TILES + 4
    ROW = D + E
    RING = 4
    OH = 4
    assert B % 2 == 0 and TILES % 2 == 0 and TILES <= 2 * P and E <= 32

    rows = nc.dram_tensor("rows", [N + P, ROW], F32, kind="Internal").ap()

    with ExitStack() as ctx:
        def sb(name, shape, dt=F32):
            return ctx.enter_context(nc.sbuf_tensor(name, shape, dt))

        def ps(name, shape, dt=F32):
            return ctx.enter_context(nc.psum_tensor(name, shape, dt))

        def sem(name):
            return ctx.enter_context(nc.semaphore(name))

        x_in = [sb(f"x_in{q}", [P, TT, D]) for q in range(2)]
        w1_in = [sb(f"w1_in{q}", [P, DC, D]) for q in range(2)]
        w2_in = [sb(f"w2_in{q}", [P, DC, I]) for q in range(2)]
        act = sb("act", [P, TT, D])
        cmax = sb("cmax", [P, 2, D])
        scaled = sb("scaled", [P, 2, TT, D])
        rounded = sb("rounded", [P, 2, TT, D])
        qT = sb("qT", [P, 2, DC, T], BF16)
        wscale_b = sb("wscale_b", [P, D])
        h = sb("h", [P, TT, D])
        sg = sb("sg", [P, TT, I])
        x2 = sb("x2", [P, TT, D])
        x2n = sb("x2n", [P, TT, D])
        x2nT = sb("x2nT", [P, DC, T])
        bn = sb("bn", [P, TT, 6])
        mv = sb("mv", [P, TT, 2])
        veps = sb("veps", [P, TT])
        rstd = sb("rstd", [P, TT])
        am = sb("am", [P, 2, DC])
        ramw = sb("ramw", [P, DC])
        ratio = sb("ratio", [P, DC])
        root = sb("root", [P, DC])
        rroot = sb("rroot", [P, DC])
        s_new = sb("s_new", [P, DC])
        sv = sb("sv", [P, 2, DC])
        rmax = sb("rmax", [P, 2, TT])
        rscale = sb("rscale", [P, 2, TT])
        rq = sb("rq", [P, 2, TT])
        half = sb("half", [P, 8])
        neghalf = sb("neghalf", [P, 8])
        magic = sb("magic", [P, 1])
        nmagic = sb("nmagic", [P, 1])
        gates = sb("gates", [P, 2])
        tg = sb("tg", [P, 2])
        ident = sb("ident", [P, P])
        gwT = sb("gwT", [P, DC, E])
        zrow = sb("zrow", [P, ROW])
        L = sb("L", [P, TT, E])
        Lc = sb("Lc", [P, TT, E])
        eL = sb("eL", [P, TT, E])
        sumL = sb("sumL", [P, TT])
        rsumL = sb("rsumL", [P, TT])
        top = sb("top", [P, TT, TOP_K])
        topc = sb("topc", [P, TT, TOP_K])
        idx = sb("idx", [P, TT, TOP_K], U32)
        idxf = sb("idxf", [P, TT, TOP_K])
        tv = sb("tv", [P, TT, TOP_K])
        ssum = sb("ssum", [P, TT])
        rsum = sb("rsum", [P, TT])
        ren = sb("ren", [P, TT, TOP_K])
        cum = sb("cum", [P, TT, TOP_K])
        carry = sb("carry", [P, TT, TOP_K])
        active = sb("active", [P, NK, TOP_K])
        rw = sb("rw", [P, TT, TOP_K])
        onehot = sb("onehot", [P, NK, TOP_K, E], BF16)
        prod = sb("prod", [P, TT, TOP_K, E])
        comb = sb("comb", [P, TT, E])
        member = sb("member", [P, NK, E], BF16)
        iota_e = sb("iota_e", [P, E])
        tri = sb("tri", [P, P], BF16)
        ones = sb("ones", [P, P], BF16)
        spare = scaled[:].rearrange("p g t d -> p (g t d)")
        tot, pre_a, pre_b, slot_e = (spare[:, n * NK * E:(n + 1) * NK * E].rearrange("p (k e) -> p k e", e=E) for n in range(4))
        pre = [pre_a, pre_b]
        cnt_i = sb("cnt_i", [P, E], I32)
        tiles_f = sb("tiles_f", [P, E])
        tend = sb("tend", [P, E])
        tend_i = sb("tend_i", [P, E], I32)
        trips_i = sb("trips_i", [P, 1], I32)
        base_e = sb("base_e", [P, E])
        one_e = sb("one_e", [P, E])
        pidx = sb("pidx", [P, 2])
        eid_c = sb("eid_c", [P, 2])
        cmp = sb("cmp", [P, E])
        eid_f = sb("eid_f", [P, 2 * P])
        eid_i = sb("eid_i", [P, 2 * P], I32)
        slot_f = sb("slot_f", [P, NK, TOP_K])
        slot_i = sb("slot_i", [P, NK * TOP_K], I32)
        lo_i = sb("lo_i", [P, NK * TOP_K], I32)
        hi_i = sb("hi_i", [P, NK * TOP_K], I32)
        lo_f = sb("lo_f", [P, NK * TOP_K])
        hi_f = sb("hi_f", [P, NK * TOP_K])
        iota_lo = sb("iota_lo", [P, P], FP16)
        iota_hi = sb("iota_hi", [P, TILES], FP16)
        label = sb("label", [P, NK])
        oh_lo = sb("oh_lo", [P, OH, P], FP16)
        oh_hi = sb("oh_hi", [P, OH, TILES], FP16)
        pad = sb("pad", [P, TILES])
        tok_f = sb("tok_f", [P, TABW])
        tok_i = sb("tok_i", [P, TABW], I32)
        wgu = sb("wgu", [P, RING, DC, GU])
        wd = sb("wd", [P, RING, 2, D])
        tok_now = [sb(f"tok_now{q}", [P, 4], I32) for q in range(2)]
        tok_out = [sb(f"tok_out{q}", [P, 4], I32) for q in range(2)]
        got = [sb(f"got{q}", [P, ROW]) for q in range(2)]
        wt = sb("wt", [P, TABW])
        pick = [sb(f"pick{q}", [P, E]) for q in range(2)]
        spare = rounded[:].rearrange("p g t d -> p (g t d)")
        at = [0]

        def carve(n):
            at[0] += n
            return spare[:, at[0] - n:at[0]]

        gT = [carve(DC * P).rearrange("p (c t) -> p c t", c=DC) for q in range(2)]
        gs = [carve(F) for q in range(2)]
        hh = [carve(F) for q in range(2)]
        hT = [carve(2 * P).rearrange("p (c t) -> p c t", c=2) for q in range(2)]
        yy = [carve(D) for q in range(2)]

        pA = [ps(f"pA{i}", [P, 512]) for i in range(2)]
        pB = [ps(f"pB{i}", [P, 512]) for i in range(2)]
        pT = [ps(f"pT{i}", [P, 512]) for i in range(2)]
        pH = [ps(f"pH{i}", [P, 512]) for i in range(2)]

        consts_loaded = sem("consts_loaded")
        pool_consts = sem("pool_consts")
        act_consts = sem("act_consts")
        x_loaded = [sem(f"x_loaded{q}") for q in range(2)]
        w1_loaded = [sem(f"w1_loaded{q}") for q in range(2)]
        w2_loaded = [sem(f"w2_loaded{q}") for q in range(2)]
        vec = sem("vec")
        var_ready = sem("var_ready")
        rstd_ready = sem("rstd_ready")
        cmax_ready = sem("cmax_ready")
        cmaxT_ready = sem("cmaxT_ready")
        ratio_ready = sem("ratio_ready")
        root_ready = sem("root_ready")
        s_ready = sem("s_ready")
        bcast_ready = sem("bcast_ready")
        scaled_ready = sem("scaled_ready")
        is_rounded = sem("is_rounded")
        staged = sem("staged")
        unstaged = sem("unstaged")
        wscale_ready = sem("wscale_ready")
        wscale_copied = sem("wscale_copied")
        product = sem("product")
        product_used = sem("product_used")
        silu_ready = sem("silu_ready")
        x2_ready = sem("x2_ready")
        x2n_ready = sem("x2n_ready")
        logits_ready = sem("logits_ready")
        logits_copied = sem("logits_copied")
        shifted = sem("shifted")
        exp_ready = sem("exp_ready")
        comb_ready = sem("comb_ready")
        x2_stored = sem("x2_stored")
        x2n_stored = sem("x2n_stored")
        comb_stored = sem("comb_stored")
        member_ready = sem("member_ready")
        ranks_ready = sem("ranks_ready")
        eid_ready = sem("eid_ready")
        eidT_ready = sem("eidT_ready")
        plan_ready = sem("plan_ready")
        hot_ready = sem("hot_ready")
        hot_used = sem("hot_used")
        tab_ready = sem("tab_ready")
        tok_ready = sem("tok_ready")
        w_landed = [sem(f"w_landed{r}") for r in range(RING)]
        weights_ready = sem("weights_ready")
        passed = sem("passed")
        out_idx_ready = sem("out_idx_ready")
        idx_ready = sem("idx_ready")
        gathered = [sem(f"gathered{q}") for q in range(2)]
        gT_filled = sem("gT_filled")
        gT_ready = sem("gT_ready")
        gu_ready = sem("gu_ready")
        gs_ready = sem("gs_ready")
        hh_ready = sem("hh_ready")
        wt_ready = sem("wt_ready")
        hT_filled = sem("hT_filled")
        hT_ready = sem("hT_ready")
        y_filled = sem("y_filled")
        y_ready = sem("y_ready")
        added = [sem(f"added{q}") for q in range(2)]
        additions = sem("additions")

        STAGES = ((DC, D), (IC, I))

        block = ctx.enter_context(nc.Block())

        @block.sync
        def _(sp):
            sp.dma_start(gwT[:], gate_w.rearrange("(c p) e -> p c e", p=P)).then_inc(consts_loaded, 16)
            sp.dma_start(gates[:, 0:1], g_x).then_inc(consts_loaded, 16)
            sp.dma_start(gates[:, 1:2], g_f).then_inc(consts_loaded, 16)

            def load(b, q):
                sp.dma_start(x_in[q][:], x[bass.ds(b, 1)].rearrange("a (t p) d -> p (a t) d", p=P)).then_inc(x_loaded[q], 16)
                sp.dma_start(w1_in[q][:], w1[bass.ds(b, 1)].rearrange("a (t p) d -> p (a t) d", p=P)).then_inc(w1_loaded[q], 16)
                sp.dma_start(w2_in[q][:], w2[bass.ds(b, 1)].rearrange("a (t p) d -> p (a t) d", p=P)).then_inc(w2_loaded[q], 16)

            def store(b):
                sp.wait_ge(x2_ready, TT * b + TT)
                sp.dma_start(out[bass.ds(b * T, T), :].rearrange("(t p) d -> p t d", p=P), x2[:]).then_inc(x2_stored, 16)
                sp.wait_ge(x2n_ready, TT * b + TT)
                sp.dma_start(rows[bass.ds(b * T, T), 0:D].rearrange("(t p) d -> p t d", p=P), x2n[:]).then_inc(x2n_stored, 16)
                sp.wait_ge(comb_ready, b + 1)
                sp.dma_start(rows[bass.ds(b * T, T), D:ROW].rearrange("(t p) d -> p t d", p=P), comb[:]).then_inc(comb_stored, 16)

            def load_expert(e, r):
                sp.dma_start(wgu[:, r], gate_up_t[bass.ds(e, 1)].rearrange("a (c p) n -> p (a c) n", p=P)).then_inc(w_landed[r], 16)
                sp.dma_start(wd[:, r, 0, :], down_t[bass.ds(e, 1), 0:P, :].rearrange("a p n -> p (a n)")).then_inc(w_landed[r], 16)
                sp.dma_start(wd[0:FREST, r, 1, :], down_t[bass.ds(e, 1), P:F, :].rearrange("a p n -> p (a n)")).then_inc(w_landed[r], 16)

            load(0, 0)
            load(1, 1)
            for r in range(RING):
                load_expert(r, r)
            with sp.Fori(0, B // 2 - 1) as it:
                for q in range(2):
                    store(2 * it + q)
                    load(2 * it + q + 2, q)
            for q in range(2):
                store(B - 2 + q)

            def announce(r, times):
                sp.wait_ge(w_landed[r], 48 * times)
                sp.sem_inc(weights_ready, 1)

            for r in range(RING - 1):
                announce(r, 1)
            sp.wait_ge(plan_ready, 1)
            with sp.Fori(0, E // RING - 1) as it:
                for r in range(RING):
                    e = it * RING + r
                    last = nc.sync.value_load(tend_i[0:1, bass.ds(e, 1)], min_val=1, max_val=TILES)
                    sp.wait_ge(y_filled, last + 2)
                    load_expert(e + RING, r)
                    announce((r - 1) % RING, it + (1 if r == 0 else 2))
            announce(RING - 1, E // RING)
            sp.wait_ge(x2_stored, 16 + 16 * B)
            sp.wait_ge(x2n_stored, 16 + 16 * B)
            sp.wait_ge(comb_stored, 16 + 16 * B)

        @block.gpsimd
        def _(pool):
            pool.memset(zrow[:], 0.0).then_inc(pool_consts, 1)
            pool.memset(half[:], 0.5).then_inc(pool_consts, 1)
            pool.memset(neghalf[:], -0.5).then_inc(pool_consts, 1)
            pool.memset(magic[:], MAGIC).then_inc(pool_consts, 1)
            pool.memset(nmagic[:], -MAGIC).then_inc(pool_consts, 1)
            pool.memset(ones[:], 1.0).then_inc(pool_consts, 1)
            pool.memset(one_e[:], 1.0).then_inc(pool_consts, 1)
            pool.memset(ident[:], 0.0).then_inc(pool_consts, 1)
            pool.memset(carry[:], 1.0).then_inc(pool_consts, 1)
            pool.iota(iota_e[:], [[1, E]], base=0, channel_multiplier=0,
                      allow_small_or_imprecise_dtypes=True).then_inc(pool_consts, 1)
            pool.iota(iota_lo[:], [[1, P]], base=0, channel_multiplier=0,
                      allow_small_or_imprecise_dtypes=True).then_inc(pool_consts, 1)
            pool.iota(iota_hi[:], [[1, TILES]], base=0, channel_multiplier=0,
                      allow_small_or_imprecise_dtypes=True).then_inc(pool_consts, 1)
            pool.iota(pidx[:], [[P, 2]], base=0, channel_multiplier=1,
                      allow_small_or_imprecise_dtypes=True).then_inc(pool_consts, 1)
            pool.iota(label[:], [[-P, NK]], base=N, channel_multiplier=-1,
                      allow_small_or_imprecise_dtypes=True).then_inc(pool_consts, 1)
            pool.wait_ge(pool_consts, 14)
            pool.affine_select(out=ident[:], in_=ident[:], compare_op=ALU.not_equal, fill=1.0,
                               base=0, pattern=[[-1, P]], channel_multiplier=1).then_inc(pool_consts, 1)
            pool.affine_select(out=tri[:], in_=ones[:], compare_op=ALU.is_gt, fill=0.0,
                               base=0, pattern=[[1, P]], channel_multiplier=-1).then_inc(pool_consts, 1)
            pool.affine_select(out=carry[:], in_=carry[:], compare_op=ALU.not_equal, fill=0.0,
                               base=0, pattern=[[0, TT], [1, TOP_K]], channel_multiplier=0).then_inc(pool_consts, 1)

            pool.dma_start(rows[N:N + P, :], zrow[:]).then_inc(added[0], 16)
            pool.dma_start(out[N:N + P, :], zrow[:, 0:D]).then_inc(added[1], 16)

            def inverse_std(b, n):
                pool.wait_ge(var_ready, 2 * b + n + 1)
                pool.tensor_tensor(rstd[:], veps[:], neghalf[:, 0:TT], ALU.pow).then_inc(rstd_ready, 1)

            def square_root(b, n):
                C = STAGES[n][0]
                pool.wait_ge(ratio_ready, 2 * b + n + 1)
                pool.tensor_tensor(root[:, 0:C], ratio[:, 0:C], half[:, 0:C], ALU.pow).then_inc(root_ready, 1)

            with pool.Fori(0, B // 2) as it:
                for q in range(2):
                    b = 2 * it + q
                    inverse_std(b, 0)
                    square_root(b, 0)
                    square_root(b, 1)
                    pool.wait_ge(x2_stored, 16 * b + 16)
                    for t in range(TT):
                        pool.wait_ge(product_used, 8 * b + TT + t + 3)
                        pool.tensor_tensor(x2[:, t, :], h[:, t, :], x_in[q][:, t, :], ALU.add).then_inc(x2_ready, 1)
                    inverse_std(b, 1)

            pool.wait_ge(tok_ready, 1)
            pool.wait_ge(x2_stored, 16 + 16 * B)
            pool.wait_ge(x2n_stored, 16 + 16 * B)
            pool.wait_ge(comb_stored, 16 + 16 * B)
            pool.wait_ge(added[0], 16)
            pool.wait_ge(added[1], 16)

            def gather(i, q):
                pool.tensor_copy(tok_now[q][:, 0:1], tok_i[:, bass.ds(i, 1)]).then_inc(idx_ready, 1)
                pool.wait_ge(idx_ready, i + 1)
                pool.sem_inc(passed, 1)
                pool.indirect_dma_start(out=got[q][:], out_offset=None, in_=rows,
                                        in_offset=bass.IndirectOffsetOnAxis(ap=tok_now[q][:, 0:1], axis=0)
                                        ).then_inc(gathered[q], 16)

            def add_rows(i, q, before):
                pool.wait_ge(added[1 - q], before)
                pool.sem_inc(additions, 1)
                pool.tensor_copy(tok_out[q][:, 0:1], tok_i[:, bass.ds(i, 1)]).then_inc(out_idx_ready, 1)
                pool.wait_ge(out_idx_ready, i + 1)
                pool.wait_ge(y_ready, i + 3)
                pool.sem_inc(passed, 1)
                pool.indirect_dma_start(out=out, out_offset=bass.IndirectOffsetOnAxis(ap=tok_out[q][:, 0:1], axis=0),
                                        in_=yy[q], in_offset=None, compute_op=ALU.add
                                        ).then_inc(added[q], 16)

            pool.sem_inc(additions, 1)
            gather(0, 0)
            gather(1, 1)
            for i in range(2):
                pool.wait_ge(gT_filled, i + 1)
                pool.wait_ge(wt_ready, i + 1)
                gather(i + 2, i)
            trips = nc.gpsimd.value_load(trips_i[0:1, 0:1], min_val=1, max_val=TILES // 2)
            with pool.Fori(0, trips) as it:
                for q in range(2):
                    i = 2 * it + q
                    pool.wait_ge(gT_filled, i + 3)
                    pool.wait_ge(wt_ready, i + 3)
                    gather(i + 4, q)
                    add_rows(i, q, 16 * it + 16 * (q + 1))
            pool.wait_ge(added[0], 16 * trips + 16)
            pool.wait_ge(added[1], 16 * trips + 16)
            pool.wait_ge(gathered[0], 16 * trips + 32)
            pool.wait_ge(gathered[1], 16 * trips + 32)

        @block.scalar
        def _(act_e):
            act_e.sem_inc(unstaged, 2)
            act_e.sem_inc(y_ready, 2)
            act_e.wait_ge(consts_loaded, 48)
            nc.scalar.activation(tg[:], gates[:], ACT.Tanh).then_inc(act_consts, 1)
            act_e.wait_ge(act_consts, 1)
            act_e.wait_ge(pool_consts, 5)

            def round_rows(b, n):
                W = STAGES[n][1]
                act_e.wait_ge(scaled_ready, 2 * b + n + 1)
                for g in range(2):
                    for t in range(TT):
                        nc.scalar.activation(rounded[:, g, t, 0:W], scaled[:, g, t, 0:W], ACT.Identity,
                                             bias=magic[:, 0:1], scale=rq[:, g, t:t + 1]).then_inc(is_rounded, 1)

            def unstage(n, b, first):
                C = STAGES[n][0]
                for g in range(2):
                    for c in range(C):
                        k = first + g * C + c
                        act_e.wait_ge(staged, 16 * b + k + 1)
                        nc.scalar.activation(qT[:, g, c, :], pT[k % 2][:], ACT.Identity,
                                             bias=nmagic[:, 0:1], scale=1.0).then_inc(unstaged, 1)

            def weight_scales(b, n):
                act_e.wait_ge(wscale_ready, 2 * b + n + 1)
                if n == 0:
                    nc.scalar.activation(wscale_b[:], pB[0][:], ACT.Copy).then_inc(wscale_copied, 1)
                else:
                    nc.scalar.activation(wscale_b[:], pB[0][:], ACT.Copy, scale=tg[:, 0:1]).then_inc(wscale_copied, 1)

            with act_e.Fori(0, B) as b:
                round_rows(b, 0)
                weight_scales(b, 0)
                unstage(0, b, 0)
                for t in range(TT):
                    act_e.wait_ge(product_used, 8 * b + t + 3)
                    nc.scalar.activation(sg[:, t, :], h[:, t, 0:I], ACT.Silu).then_inc(silu_ready, 1)
                round_rows(b, 1)
                weight_scales(b, 1)
                unstage(1, b, 2 * DC)
                for c in range(DC):
                    k = 2 * DC + 2 * IC + c
                    act_e.wait_ge(staged, 16 * b + k + 1)
                    nc.scalar.activation(x2nT[:, c, :], pT[k % 2][:], ACT.Copy).then_inc(unstaged, 1)
                act_e.wait_ge(logits_ready, b + 1)
                nc.scalar.activation(L[:], pA[0][:, 0:TT * E].rearrange("p (t e) -> p t e", e=E), ACT.Copy).then_inc(logits_copied, 1)
                act_e.wait_ge(shifted, b + 1)
                nc.scalar.activation(eL[:], Lc[:], ACT.Exp).then_inc(exp_ready, 1)
                nc.scalar.activation(tv[:], topc[:], ACT.Exp).then_inc(exp_ready, 1)

            act_e.wait_ge(tok_ready, 1)

            def rows_across(i, q):
                act_e.wait_ge(gT_filled, i + 1)
                nc.scalar.activation(gT[q], pT[q][:].rearrange("p (c t) -> p c t", c=DC), ACT.Copy).then_inc(gT_ready, 1)

            def silu_gate(i, q):
                act_e.wait_ge(gu_ready, i + 1)
                nc.scalar.activation(gs[q], pH[q][:, 0:F], ACT.Silu).then_inc(gs_ready, 1)

            def weigh_rows(i, q):
                act_e.wait_ge(y_filled, i + 3)
                act_e.wait_ge(additions, i + 1)
                nc.scalar.activation(yy[q], pB[q][:], ACT.Copy, scale=wt[:, bass.ds(i, 1)]).then_inc(y_ready, 1)

            trips = nc.scalar.value_load(trips_i[0:1, 0:1], min_val=1, max_val=TILES // 2)
            rows_across(0, 0)
            rows_across(1, 1)
            silu_gate(0, 0)
            with act_e.Fori(0, trips) as it:
                for i, q in ((2 * it + 1, 1), (2 * it + 2, 0)):
                    rows_across(i + 1, 1 - q)
                    silu_gate(i, q)
                    act_e.wait_ge(wt_ready, i)
                    weigh_rows(i - 1, 1 - q)

        @block.tensor
        def _(pe):
            pe.wait_ge(pool_consts, 17)
            pe.wait_ge(consts_loaded, 48)
            pe.sem_inc(y_filled, 2)

            def column_maxima(b, n):
                C = STAGES[n][0]
                pe.wait_ge(cmax_ready, 4 * b + 2 * n + 2)
                for g in range(2):
                    for c in range(C):
                        mm = nc.tensor.transpose(pA[g][:, c * P:(c + 1) * P], cmax[:, g, c * P:(c + 1) * P], ident[:])
                mm.then_inc(cmaxT_ready, 1)

            def spread(dst, col):
                return nc.tensor.matmul(dst, col.to_broadcast([P, P]), ident[:], start=True, stop=True)

            def column_scales(b, n):
                C = STAGES[n][0]
                pe.wait_ge(s_ready, 2 * b + n + 1)
                for g in range(2):
                    for c in range(C):
                        mm = spread(pB[g][:, c * P:(c + 1) * P], sv[:, g, c:c + 1])
                mm.then_inc(bcast_ready, 1)

            def weight_scales(b, n):
                pe.wait_ge(scaled_ready, 2 * b + n + 1)
                for t in range(DC):
                    mm = spread(pB[0][:, t * P:(t + 1) * P], rscale[:, 1, t:t + 1])
                mm.then_inc(wscale_ready, 1)

            def stage_columns(b, n, first):
                C = STAGES[n][0]
                for g in range(2):
                    for c in range(C):
                        k = first + g * C + c
                        pe.wait_ge(unstaged, 16 * b + k + 1)
                        for t in range(TT):
                            if c == 0:
                                pe.wait_ge(is_rounded, 16 * b + 8 * n + 4 * g + t + 1)
                            mm = nc.tensor.transpose(pT[k % 2][:, t * P:(t + 1) * P],
                                                     rounded[:, g, t, c * P:(c + 1) * P], ident[:])
                        mm.then_inc(staged, 1)

            def products(b, n, last_staged):
                C = STAGES[n][0]
                pe.wait_ge(unstaged, 16 * b + last_staged + 2)
                for t in range(TT):
                    pe.wait_ge(product_used, 8 * b + 4 * n + t + 1)
                    for c in range(C):
                        mm = nc.tensor.matmul(pH[t % 2][:], qT[:, 0, c, t * P:(t + 1) * P], qT[:, 1, c, :],
                                              start=(c == 0), stop=(c == C - 1))
                    mm.then_inc(product, 1)

            with pe.Fori(0, B) as b:
                for n, first in ((0, 0), (1, 2 * DC)):
                    column_maxima(b, n)
                    column_scales(b, n)
                    weight_scales(b, n)
                    stage_columns(b, n, first)
                    products(b, n, first + 2 * STAGES[n][0])
                first = 2 * DC + 2 * IC
                for t in range(TT):
                    pe.wait_ge(x2n_ready, TT * b + t + 1)
                for c in range(DC):
                    k = first + c
                    pe.wait_ge(unstaged, 16 * b + k + 1)
                    for t in range(TT):
                        mm = nc.tensor.transpose(pT[k % 2][:, t * P:(t + 1) * P], x2n[:, t, c * P:(c + 1) * P], ident[:])
                    mm.then_inc(staged, 1)
                pe.wait_ge(unstaged, 16 * b + 18)
                for t in range(TT):
                    for c in range(DC):
                        mm = nc.tensor.matmul(pA[0][:, t * E:(t + 1) * E], x2nT[:, c, t * P:(t + 1) * P], gwT[:, c, :],
                                              start=(c == 0), stop=(c == DC - 1))
                mm.then_inc(logits_ready, 1)

            pe.wait_ge(comb_ready, B)
            mflat = member[:].rearrange("p k e -> p (k e)")
            nc.tensor.matmul(pA[0][:], tri[:], mflat, start=True, stop=True)
            nc.tensor.matmul(pA[1][:], ones[:], mflat, start=True, stop=True).then_inc(ranks_ready, 1)
            pe.wait_ge(eid_ready, 1)
            for g in range(2):
                mm = spread(pB[0][:, g * P:(g + 1) * P], eid_c[:, g:g + 1])
            mm.then_inc(eidT_ready, 1)
            zero_lo, zero_hi = zrow[:, 0:P // 2].bitcast(FP16), zrow[:, 0:TILES // 2].bitcast(FP16)
            nc.tensor.matmul(pB[1][:, 0:TILES], zero_lo, zero_hi, start=True, stop=False, skip_group_check=True)
            with pe.Fori(0, NK) as k:
                for j in range(TOP_K):
                    pe.wait_ge(hot_ready, TOP_K * k + j + 1)
                    nc.tensor.matmul(pB[1][:, 0:TILES], oh_lo[:, j % OH, :], oh_hi[:, j % OH, :],
                                     start=False, stop=False, skip_group_check=True).then_inc(hot_used, 1)
            nc.tensor.matmul(pB[1][:, 0:TILES], zero_lo, zero_hi, start=False, stop=True,
                             skip_group_check=True).then_inc(tab_ready, 1)

            pe.wait_ge(tok_ready, 1)

            def rows_across(i, q):
                if q == 0:
                    pe.wait_ge(gathered[0], 8 * i + 16)
                else:
                    pe.wait_ge(gathered[1], 8 * i + 8)
                for c in range(DC):
                    mm = nc.tensor.transpose(pT[q][:, c * P:(c + 1) * P], got[q][:, c * P:(c + 1) * P], ident[:])
                mm.then_inc(gT_filled, 1)

            def gate_up(i, q):
                e = nc.tensor.value_load(eid_i[0:1, bass.ds(i, 1)], min_val=0, max_val=E - 1)
                slot = nc.tensor.snap(e % RING, min_val=0, max_val=RING - 1)
                pe.wait_ge(weights_ready, e + 1)
                pe.wait_ge(gT_ready, i + 1)
                for c in range(DC):
                    mm = nc.tensor.matmul(pH[q][:, 0:GU], gT[q][:, c, :], wgu[:, bass.ds(slot, 1), c, :],
                                          start=(c == 0), stop=(c == DC - 1))
                mm.then_inc(gu_ready, 1)

            def inner_across(i, q):
                pe.wait_ge(hh_ready, i + 1)
                nc.tensor.transpose(pA[q][:, 0:P], hh[q][:, 0:P], ident[:])
                nc.tensor.transpose(pA[q][0:FREST, P:2 * P], hh[q][:, P:F], ident[:]).then_inc(hT_filled, 1)

            def down(i, q):
                e = nc.tensor.value_load(eid_i[0:1, bass.ds(i, 1)], min_val=0, max_val=E - 1)
                slot = nc.tensor.snap(e % RING, min_val=0, max_val=RING - 1)
                pe.wait_ge(hT_ready, i + 1)
                pe.wait_ge(y_ready, i + 1)
                nc.tensor.matmul(pB[q][:], hT[q][:, 0, :], wd[:, bass.ds(slot, 1), 0, :], start=True, stop=False)
                nc.tensor.matmul(pB[q][:], hT[q][0:FREST, 1, :], wd[0:FREST, bass.ds(slot, 1), 1, :],
                                 start=False, stop=True).then_inc(y_filled, 1)

            trips = nc.tensor.value_load(trips_i[0:1, 0:1], min_val=1, max_val=TILES // 2)
            rows_across(0, 0)
            rows_across(1, 1)
            gate_up(0, 0)
            with pe.Fori(0, trips) as it:
                for i, q in ((2 * it + 1, 1), (2 * it + 2, 0)):
                    pe.wait_ge(gT_ready, i)
                    rows_across(i + 1, 1 - q)
                    inner_across(i - 1, 1 - q)
                    gate_up(i, q)
                    down(i - 1, 1 - q)

        @block.vector
        def _(dve):
            count = [0, 0, 0]

            def step(ins):
                count[0] += 1
                return ins.then_inc(vec, 1)

            def settle():
                dve.wait_ge(vec, count[1] * count[2] + count[0])

            dve.sem_inc(product_used, 2)
            dve.sem_inc(hot_used, OH)
            dve.sem_inc(x2_stored, 16)
            dve.sem_inc(x2n_stored, 16)
            dve.sem_inc(comb_stored, 16)
            dve.wait_ge(pool_consts, 17)

            def layer_norm(src, dst, b, n):
                for t in range(TT):
                    if n == 1:
                        dve.wait_ge(x2_ready, TT * b + t + 1)
                    step(nc.vector.bn_stats(bn[:, t, :], src[:, t, :]))
                settle()
                dve.sem_inc(passed, 1)
                for t in range(TT):
                    step(nc.vector.bn_aggr(mv[:, t, :], bn[:, t, :]))
                settle()
                nc.vector.tensor_scalar(veps[:], mv[:, :, 1], EPS_LN, None, ALU.add).then_inc(var_ready, 1)
                dve.wait_ge(rstd_ready, 2 * b + n + 1)
                if n == 1:
                    dve.wait_ge(x2n_stored, 16 * b + 16)
                for t in range(TT):
                    ins = nc.vector.tensor_scalar(dst[:, t, :], src[:, t, :], mv[:, t, 0:1], rstd[:, t:t + 1],
                                                  ALU.subtract, ALU.mult)
                    if n == 0:
                        step(ins)
                    else:
                        ins.then_inc(x2n_ready, 1)

            def quantise(wsrc, b, n):
                C, W = STAGES[n]
                settle()
                for g, src in ((0, act), (1, wsrc)):
                    nc.vector.tensor_reduce(cmax[:, g, 0:W], src[:, :, 0:W].rearrange("p t d -> p d t"), AX.X, ALU.max,
                                            apply_absolute_value=True).then_inc(cmax_ready, 1)
                dve.wait_ge(cmaxT_ready, 2 * b + n + 1)
                for g in range(2):
                    step(nc.vector.tensor_reduce(am[:, g, 0:C], pA[g][:, 0:W].rearrange("p (c t) -> p c t", t=P),
                                                 AX.X, ALU.max))
                settle()
                step(nc.vector.tensor_scalar(am[:, :, 0:C], am[:, :, 0:C], EPS_Q, None, ALU.max))
                settle()
                step(nc.vector.reciprocal(ramw[:, 0:C], am[:, 1, 0:C]))
                settle()
                nc.vector.tensor_tensor(ratio[:, 0:C], am[:, 0, 0:C], ramw[:, 0:C], ALU.mult).then_inc(ratio_ready, 1)
                dve.wait_ge(root_ready, 2 * b + n + 1)
                step(nc.vector.reciprocal(rroot[:, 0:C], root[:, 0:C]))
                settle()
                step(nc.vector.tensor_tensor(rroot[:, 0:C], ratio[:, 0:C], rroot[:, 0:C], ALU.mult))
                settle()
                step(nc.vector.tensor_tensor(s_new[:, 0:C], root[:, 0:C], rroot[:, 0:C], ALU.add))
                settle()
                step(nc.vector.tensor_scalar(sv[:, 1, 0:C], s_new[:, 0:C], 0.5, EPS_Q, ALU.mult, ALU.max))
                settle()
                nc.vector.reciprocal(sv[:, 0, 0:C], sv[:, 1, 0:C]).then_inc(s_ready, 1)
                dve.wait_ge(bcast_ready, 2 * b + n + 1)
                for g, src in ((0, act), (1, wsrc)):
                    step(nc.vector.tensor_tensor(scaled[:, g, :, 0:W], src[:, :, 0:W],
                                                 pB[g][:, 0:W].unsqueeze(1).to_broadcast([P, TT, W]), ALU.mult))
                settle()
                for g in range(2):
                    step(nc.vector.tensor_reduce(rmax[:, g, :], scaled[:, g, :, 0:W], AX.X, ALU.max,
                                                 apply_absolute_value=True))
                settle()
                step(nc.vector.tensor_scalar(rscale[:], rmax[:], EPS_Q, 1.0 / QMAX, ALU.max, ALU.mult))
                settle()
                nc.vector.reciprocal(rq[:], rscale[:]).then_inc(scaled_ready, 1)
                dve.wait_ge(wscale_copied, 2 * b + n + 1)

            def dequantise(b, n):
                for t in range(TT):
                    dve.wait_ge(product, 8 * b + 4 * n + t + 1)
                    nc.vector.scalar_tensor_tensor(out=h[:, t, :], in0=pH[t % 2][:], scalar=rscale[:, 0, t:t + 1],
                                                   in1=wscale_b[:], op0=ALU.mult, op1=ALU.mult).then_inc(product_used, 1)

            def route(b):
                k0 = TT * b
                dve.wait_ge(logits_copied, b + 1)
                dve.sem_inc(passed, 1)
                for t in range(TT):
                    step(nc.vector.max(top[:, t, :], L[:, t, :]))
                settle()
                dve.sem_inc(passed, 1)
                for t in range(TT):
                    step(nc.vector.max_index(idx[:, t, :], top[:, t, :], L[:, t, :]))
                first = top[:, :, 0:1]
                step(nc.vector.tensor_tensor(Lc[:], L[:], first.to_broadcast([P, TT, E]), ALU.subtract))
                nc.vector.tensor_tensor(topc[:], top[:], first.to_broadcast([P, TT, TOP_K]), ALU.subtract).then_inc(shifted, 1)
                settle()
                step(nc.vector.tensor_copy(idxf[:], idx[:]))
                settle()
                step(nc.vector.tensor_tensor(
                    onehot[:, bass.ds(k0, TT), :, :],
                    iota_e[:].unsqueeze(1).unsqueeze(1).to_broadcast([P, TT, TOP_K, E]),
                    idxf[:].unsqueeze(3).to_broadcast([P, TT, TOP_K, E]), ALU.is_equal))
                dve.wait_ge(exp_ready, 2 * b + 2)
                step(nc.vector.tensor_reduce(sumL[:], eL[:], AX.X, ALU.add))
                settle()
                step(nc.vector.reciprocal(rsumL[:], sumL[:]))
                settle()
                step(nc.vector.tensor_tensor(tv[:], tv[:], rsumL[:].unsqueeze(2).to_broadcast([P, TT, TOP_K]), ALU.mult))
                settle()

                def normalised(dst, src):
                    step(nc.vector.tensor_reduce(ssum[:], src, AX.X, ALU.add))
                    settle()
                    step(nc.vector.tensor_scalar(ssum[:], ssum[:], SUM_FLOOR, None, ALU.max))
                    settle()
                    step(nc.vector.reciprocal(rsum[:], ssum[:]))
                    settle()
                    step(nc.vector.tensor_tensor(dst, src, rsum[:].unsqueeze(2).to_broadcast([P, TT, TOP_K]), ALU.mult))
                    settle()

                normalised(ren[:], tv[:])
                step(nc.vector.tensor_tensor_scan(cum[:].rearrange("p t j -> p (t j)"), carry[:].rearrange("p t j -> p (t j)"),
                                                  ren[:].rearrange("p t j -> p (t j)"), 0.0, ALU.mult, ALU.add))
                settle()
                step(nc.vector.tensor_scalar(active[:, bass.ds(k0, TT), 1:TOP_K], cum[:, :, 0:TOP_K - 1], THRESHOLD, None, ALU.is_lt))
                settle()
                step(nc.vector.tensor_tensor(rw[:], tv[:], active[:, bass.ds(k0, TT), :], ALU.mult))
                settle()
                normalised(rw[:], rw[:])
                step(nc.vector.tensor_tensor(prod[:], onehot[:, bass.ds(k0, TT), :, :],
                                             rw[:].unsqueeze(3).to_broadcast([P, TT, TOP_K, E]), ALU.mult))
                settle()
                step(nc.vector.tensor_reduce(eL[:], prod[:].rearrange("p t j e -> p t e j"), AX.X, ALU.add))
                settle()
                step(nc.vector.tensor_tensor(prod[:], onehot[:, bass.ds(k0, TT), :, :],
                                             active[:, bass.ds(k0, TT), :].unsqueeze(3).to_broadcast([P, TT, TOP_K, E]), ALU.mult))
                settle()
                dve.wait_ge(comb_stored, 16 * b + 16)
                step(nc.vector.tensor_scalar(comb[:], eL[:], tg[:, 1:2], None, ALU.mult))
                nc.vector.tensor_reduce(member[:, bass.ds(k0, TT), :], prod[:].rearrange("p t j e -> p t e j"),
                                        AX.X, ALU.max).then_inc(comb_ready, 1)

            def entry(b, q, it):
                dve.wait_ge(x_loaded[q], 16 * it + 16)
                layer_norm(x_in[q], act, b, 0)
                dve.wait_ge(w1_loaded[q], 16 * it + 16)
                quantise(w1_in[q], b, 0)
                dequantise(b, 0)
                for t in range(TT):
                    dve.wait_ge(silu_ready, TT * b + t + 1)
                    step(nc.vector.tensor_tensor(act[:, t, 0:I], sg[:, t, :], h[:, t, I:2 * I], ALU.mult))
                dve.wait_ge(w2_loaded[q], 16 * it + 16)
                quantise(w2_in[q], b, 1)
                dequantise(b, 1)
                layer_norm(x2, x2n, b, 1)
                route(b)

            dve.wait_ge(act_consts, 1)
            nc.vector.memset(active[:], 1.0)
            count[2] = STEPS_PER_PASS
            with dve.Fori(0, B // 2) as it:
                count[1] = it
                for q in range(2):
                    entry(2 * it + q, q, it)
                assert count[0] == STEPS_PER_PASS, count
            count[:] = [B // 2 * STEPS_PER_PASS, 0, 0]

            dve.wait_ge(comb_ready, B)
            dve.wait_ge(ranks_ready, 1)
            step(nc.vector.tensor_copy(tot, pA[1][:].rearrange("p (k e) -> p k e", e=E)))
            settle()
            src, d, flip = tot, 1, 0
            while d < NK:
                dst = pre[flip]
                step(nc.vector.tensor_copy(dst[:, 0:d, :], src[:, 0:d, :]))
                step(nc.vector.tensor_tensor(dst[:, d:NK, :], src[:, d:NK, :], src[:, 0:NK - d, :], ALU.add))
                settle()
                src, d, flip = dst, 2 * d, 1 - flip
            step(nc.vector.tensor_scalar(cnt_i[:], src[:, NK - 1, :], float(P - 1), None, ALU.add))
            settle()
            step(nc.vector.tensor_scalar(tend_i[:], cnt_i[:], 7, None, ALU.logical_shift_right))
            settle()
            step(nc.vector.tensor_scalar(tiles_f[:], tend_i[:], 1.0, None, ALU.max))
            settle()
            step(nc.vector.tensor_tensor_scan(tend[:], one_e[:], tiles_f[:], 0.0, ALU.mult, ALU.add))
            settle()
            step(nc.vector.tensor_copy(tend_i[:], tend[:]))
            step(nc.vector.tensor_scalar(cnt_i[:, 0:1], tend[:, E - 1:E], 1.0, None, ALU.add))
            for g in range(2):
                step(nc.vector.tensor_scalar(cmp[:], tend[:], pidx[:, g:g + 1], None, ALU.is_le))
                settle()
                step(nc.vector.tensor_reduce(eid_c[:, g:g + 1], cmp[:], AX.X, ALU.add))
                settle()
            nc.vector.tensor_scalar(eid_c[:], eid_c[:], float(E - 1), None, ALU.min).then_inc(eid_ready, 1)
            step(nc.vector.tensor_scalar(trips_i[:], cnt_i[:, 0:1], 1, None, ALU.logical_shift_right))
            step(nc.vector.tensor_tensor(base_e[:], tend[:], tiles_f[:], ALU.subtract))
            step(nc.vector.tensor_tensor(slot_e, src[:], tot, ALU.subtract))
            settle()
            step(nc.vector.tensor_tensor(slot_e, slot_e, pA[0][:].rearrange("p (k e) -> p k e", e=E), ALU.add))
            settle()
            step(nc.vector.scalar_tensor_tensor(out=slot_e, in0=base_e[:].unsqueeze(1).to_broadcast([P, NK, E]), scalar=float(P),
                                                in1=slot_e, op0=ALU.mult, op1=ALU.add))
            dve.wait_ge(eidT_ready, 1)
            step(nc.vector.tensor_copy(eid_f[:], pB[0][:, 0:2 * P]))
            step(nc.vector.tensor_copy(eid_i[:], pB[0][:, 0:2 * P]))
            settle()
            for k in range(0, NK, TT):
                step(nc.vector.tensor_tensor(prod[:], onehot[:, k:k + TT, :, :],
                                             slot_e[:, k:k + TT, :].unsqueeze(2).to_broadcast([P, TT, TOP_K, E]), ALU.mult))
                settle()
                step(nc.vector.tensor_reduce(slot_f[:, k:k + TT, :], prod[:], AX.X, ALU.add))
                settle()
            step(nc.vector.scalar_tensor_tensor(out=slot_f[:], in0=active[:], scalar=-32768.0, in1=slot_f[:],
                                                op0=ALU.mult, op1=ALU.add))
            settle()
            step(nc.vector.tensor_scalar(slot_i[:], slot_f[:].rearrange("p k j -> p (k j)"), 32768.0, None, ALU.add))
            settle()
            step(nc.vector.tensor_scalar(lo_i[:], slot_i[:], P - 1, None, ALU.bitwise_and))
            step(nc.vector.tensor_scalar(hi_i[:], slot_i[:], 7, None, ALU.logical_shift_right))
            settle()
            step(nc.vector.tensor_copy(lo_f[:], lo_i[:]))
            step(nc.vector.tensor_copy(hi_f[:], hi_i[:]))
            settle()
            with dve.Fori(0, NK) as k:
                for j in range(TOP_K):
                    n = TOP_K * k + j
                    dve.wait_ge(hot_used, n + 1)
                    nc.vector.tensor_scalar(oh_lo[:, j % OH, :], iota_lo[:], lo_f[:, bass.ds(n, 1)], None, ALU.is_equal)
                    nc.vector.tensor_scalar(oh_hi[:, j % OH, :], iota_hi[:], hi_f[:, bass.ds(n, 1)], label[:, bass.ds(k, 1)],
                                            ALU.is_equal, ALU.mult).then_inc(hot_ready, 1)
            dve.wait_ge(tab_ready, 1)
            step(nc.vector.tensor_scalar(pad[:], pB[1][:, 0:TILES], 0.0, pidx[:, 0:1], ALU.is_equal, ALU.mult))
            step(nc.vector.tensor_scalar(tok_f[:, 0:TILES], pB[1][:, 0:TILES], -1.0, float(N), ALU.mult, ALU.add))
            step(nc.vector.tensor_scalar(tok_i[:, TILES:TABW], one_e[:, 0:TABW - TILES], float(N), pidx[:, 0:1], ALU.mult, ALU.add))
            settle()
            nc.vector.tensor_tensor(tok_i[:, 0:TILES], tok_f[:, 0:TILES], pad[:], ALU.add).then_inc(plan_ready, 1)
            dve.wait_ge(plan_ready, 1)
            dve.sem_inc(tok_ready, 1)

            def row_weights(i, q):
                if q == 0:
                    dve.wait_ge(gathered[0], 8 * i + 16)
                else:
                    dve.wait_ge(gathered[1], 8 * i + 8)
                nc.vector.scalar_tensor_tensor(out=pick[q][:], in0=iota_e[:], scalar=eid_f[:, bass.ds(i, 1)], in1=got[q][:, D:ROW],
                                               op0=ALU.is_equal, op1=ALU.mult,
                                               accum_out=wt[:, bass.ds(i, 1)]).then_inc(wt_ready, 1)

            def inner(i, q):
                dve.wait_ge(gs_ready, i + 1)
                nc.vector.tensor_tensor(hh[q], gs[q], pH[q][:, F:GU], ALU.mult).then_inc(hh_ready, 1)

            def inner_across(i, q):
                dve.wait_ge(hT_filled, i + 1)
                dve.wait_ge(y_filled, i + 1)
                nc.vector.tensor_copy(hT[q], pA[q][:, 0:2 * P].rearrange("p (c t) -> p c t", c=2)).then_inc(hT_ready, 1)

            trips = nc.vector.value_load(trips_i[0:1, 0:1], min_val=1, max_val=TILES // 2)
            row_weights(0, 0)
            row_weights(1, 1)
            inner(0, 0)
            with dve.Fori(0, trips) as it:
                for i, q in ((2 * it + 1, 1), (2 * it + 2, 0)):
                    row_weights(i + 1, 1 - q)
                    inner_across(i - 1, 1 - q)
                    inner(i, q)


_INS = ["x", "fside_BxS2xS2_0", "ctx_1024", "g_xattn", "g_ffn", "L0_ffn_gate_weight", "L0_ffn_gate_up_proj",
        "L0_ffn_down_proj"]


def kernel(**inputs):
    import numpy as _np
    import concourse.bacc as _bacc
    from concourse import mybir as _mybir
    from concourse.bass_utils import run_bass_kernel_spmd as _run

    data = {n: _np.asarray(inputs[n]) for n in _INS}
    B, T, D = data["x"].shape
    for n in ("g_xattn", "g_ffn"):
        data[n] = _np.broadcast_to(data[n].reshape(1, 1), (P, 1))
    data["L0_ffn_gate_weight"] = data["L0_ffn_gate_weight"].T
    data["L0_ffn_gate_up_proj"] = data["L0_ffn_gate_up_proj"].transpose(0, 2, 1)
    data["L0_ffn_down_proj"] = data["L0_ffn_down_proj"].transpose(0, 2, 1)

    nc = _bacc.Bacc("TRN2", target_bir_lowering=False, num_devices=1)
    arrays, args = {}, []
    for name in _INS:
        a = _np.ascontiguousarray(data[name])
        arrays[f"in_{name}"] = a
        args.append(nc.dram_tensor(f"in_{name}", a.shape, _mybir.dt.from_np(a.dtype), kind="ExternalInput").ap())
    args.append(nc.dram_tensor("out_rows", (B * T + P, D), _mybir.dt.from_np(_np.dtype("float32")), kind="ExternalOutput").ap())
    build(nc, *args)
    r = _run(nc, [arrays], core_ids=[0])
    return r.results[0]["out_rows"][0:B * T].reshape(B, T, D)
```

```python
from contextlib import ExitStack

import concourse.bass as bass
from concourse import mybir

P = 128
STEPS_PER_PASS = 68
ALU = mybir.AluOpType
ACT = mybir.ActivationFunctionType
F32 = mybir.dt.float32
BF16 = mybir.dt.bfloat16
FP16 = mybir.dt.float16
I32 = mybir.dt.int32
U32 = mybir.dt.uint32
AX = mybir.AxisListType

EPS_Q = 1e-6
EPS_LN = 1e-5
QMAX = 127.0
MAGIC = 1.5 * 2.0 ** 23
TOP_K = 8
THRESHOLD = 0.8
SUM_FLOOR = 1e-12


class Linear:
    pass


def build(nc, x, w1, w2, g_x, g_f, gate_w, gate_up_t, down_t, out):
    B, T, D = x.shape
    I = w2.shape[2]
    E, _, GU = gate_up_t.shape
    F = GU // 2
    TT = T // P
    DC = D // P
    IC = I // P
    NK = B * TT
    N = B * T
    FREST = F - P
    TILES = N * TOP_K // P + E
    TABW = TILES + 4
    ROW = D + E
    RING = 4
    LO_BY_POOL = (1, 4, 7)
    HI_BY_ACT = (2, 4, 6)
    OH = 8
    assert B % 2 == 0 and TILES % 2 == 0 and TILES <= 2 * P and E <= 32

    rows = nc.dram_tensor("rows", [N + P, ROW], F32, kind="Internal").ap()

    with ExitStack() as ctx:
        def sb(name, shape, dt=F32):
            return ctx.enter_context(nc.sbuf_tensor(name, shape, dt))

        def ps(name, shape, dt=F32):
            return ctx.enter_context(nc.psum_tensor(name, shape, dt))

        def sem(name):
            return ctx.enter_context(nc.semaphore(name))

        x_in = sb("x_in", [P, B, TT, D])
        front = Linear()
        front.chunks = DC; front.width = D; front.at = 0
        front.w_in = sb("w1_in", [P, DC, D])
        front.cmax = sb("f_cmax", [P, 2, D])
        front.grid = sb("f_grid", [P, 2, TT, D])
        front.qT = sb("f_qT", [P, 2, DC, T], BF16)
        front.wscale = sb("f_wscale", [P, D])
        front.s_row = sb("f_s_row", [P, D])
        front.prod = sb("f_prod", [P, TT, D])
        back = Linear()
        back.chunks = IC; back.width = I; back.at = 1
        back.w_in = sb("w2_in", [P, DC, I])
        back.cmax = sb("b_cmax", [P, 2, I])
        back.grid = sb("b_grid", [P, 2, TT, I])
        back.qT = sb("b_qT", [P, 2, IC, T], BF16)
        back.wscale = sb("b_wscale", [P, D])
        back.s_row = sb("b_s_row", [P, I])
        back.prod = sb("b_prod", [P, TT, D])
        for v in (front, back):
            v.am = sb(f"am{v.at}", [P, 2, v.chunks])
            v.ramw = sb(f"ramw{v.at}", [P, v.chunks])
            v.ratio = sb(f"ratio{v.at}", [P, v.chunks])
            v.root = sb(f"root{v.at}", [P, v.chunks])
            v.rroot = sb(f"rroot{v.at}", [P, v.chunks])
            v.sv = sb(f"sv{v.at}", [P, 2, v.chunks])
            v.rmax = sb(f"rmax{v.at}", [P, 2, TT])
            v.rscale = sb(f"rscale{v.at}", [P, 2, TT])
            v.rq = sb(f"rq{v.at}", [P, 2, TT])
            v.bn = sb(f"bn{v.at}", [P, TT, 6])
            v.mv = sb(f"mv{v.at}", [P, TT, 2])
            v.veps = sb(f"veps{v.at}", [P, TT])
            v.rstd = sb(f"rstd{v.at}", [P, TT])
            v.nmr = sb(f"nmr{v.at}", [P, TT])
        sg = sb("sg", [P, TT, I])
        x2n = sb("x2n", [P, TT, D])
        x2nT = sb("x2nT", [P, TT, DC, P])
        half = sb("half", [P, 8])
        neghalf = sb("neghalf", [P, 8])
        magic = sb("magic", [P, 1])
        nmagic = sb("nmagic", [P, 1])
        gates = sb("gates", [P, 2])
        tg = sb("tg", [P, 2])
        ident = sb("ident", [P, P])
        gwT = sb("gwT", [P, DC, E])
        zrow = sb("zrow", [P, ROW])
        L = sb("L", [P, TT, E])
        Lc = sb("Lc", [P, TT, E])
        eL = sb("eL", [P, TT, E])
        sumL = sb("sumL", [P, TT])
        rsumL = sb("rsumL", [P, TT])
        top = sb("top", [P, TT, TOP_K])
        topc = sb("topc", [P, TT, TOP_K])
        idx = sb("idx", [P, TT, TOP_K], U32)
        idxf = sb("idxf", [P, TT, TOP_K])
        tv = sb("tv", [P, TT, TOP_K])
        ssum = sb("ssum", [P, TT])
        rsum = sb("rsum", [P, TT])
        ren = sb("ren", [P, TT, TOP_K])
        cum = sb("cum", [P, TT, TOP_K])
        carry = sb("carry", [P, TT, TOP_K])
        active = sb("active", [P, NK, TOP_K])
        rw = sb("rw", [P, TT, TOP_K])
        keep = sb("keep", [P, TT, TOP_K])
        onehot = sb("onehot", [P, NK, TOP_K, E], BF16)
        prod = sb("prod", [P, TT, TOP_K, E])
        comb = sb("comb", [P, TT, E])
        member = sb("member", [P, NK, E], BF16)
        iota_e = sb("iota_e", [P, E])
        tri = sb("tri", [P, P], BF16)
        ones = sb("ones", [P, P], BF16)
        spare = back.prod[:].rearrange("p t d -> p (t d)")
        tot, pre_a, pre_b, slot_e = (spare[:, n * NK * E:(n + 1) * NK * E].rearrange("p (k e) -> p k e", e=E) for n in range(4))
        pre = [pre_a, pre_b]
        cnt_i = sb("cnt_i", [P, E], I32)
        tiles_f = sb("tiles_f", [P, E])
        tend = sb("tend", [P, E])
        tend_i = sb("tend_i", [P, E], I32)
        trips_i = sb("trips_i", [P, 1], I32)
        base_e = sb("base_e", [P, E])
        one_e = sb("one_e", [P, E])
        pidx = sb("pidx", [P, 2])
        eid_c = sb("eid_c", [P, 2])
        cmp = sb("cmp", [P, E])
        eid_f = sb("eid_f", [P, 2 * P])
        eid_i = sb("eid_i", [P, 2 * P], I32)
        spare = back.grid[:].rearrange("p g t d -> p (g t d)")
        slot_f, slot_i, lo_i, hi_i, lo_f, hi_f = (spare[:, n * NK * TOP_K:(n + 1) * NK * TOP_K] for n in range(6))
        slot_f = slot_f.rearrange("p (k j) -> p k j", j=TOP_K)
        slot_i, lo_i, hi_i = slot_i.bitcast(I32), lo_i.bitcast(I32), hi_i.bitcast(I32)
        iota_lo = sb("iota_lo", [P, P], FP16)
        iota_hi = sb("iota_hi", [P, TILES], FP16)
        label = sb("label", [P, NK])
        spare = front.qT[:].rearrange("p g c t -> p (g c t)").bitcast(FP16)
        oh_lo = spare[:, 0:OH * P].rearrange("p (o n) -> p o n", n=P)
        oh_hi = spare[:, OH * P:OH * (P + TILES)].rearrange("p (o n) -> p o n", n=TILES)
        nlabel = sb("nlabel", [P, NK])
        lo_now = sb("lo_now", [P, TOP_K])
        far = front.s_row[:].bitcast(FP16)[:, 0:len(HI_BY_ACT) * TILES].rearrange("p (a n) -> p a n", n=TILES)
        pad = sb("pad", [P, TILES])
        tok_f = sb("tok_f", [P, TABW])
        tok_i = sb("tok_i", [P, TABW], I32)
        wgu = sb("wgu", [P, RING, DC, GU])
        wd = sb("wd", [P, RING, 2, D])
        tok_now = [sb(f"tok_now{q}", [P, 4], I32) for q in range(2)]
        tok_out = [sb(f"tok_out{q}", [P, 4], I32) for q in range(2)]
        got = [sb(f"got{q}", [P, ROW]) for q in range(2)]
        wt = sb("wt", [P, TABW])
        pick = [sb(f"pick{q}", [P, E]) for q in range(2)]
        spare = front.grid[:].rearrange("p g t d -> p (g t d)")
        at = [0]

        def carve(n):
            at[0] += n
            return spare[:, at[0] - n:at[0]]

        gT = [carve(DC * P).rearrange("p (c t) -> p c t", c=DC) for q in range(2)]
        gs = [carve(F) for q in range(2)]
        hh = [carve(F) for q in range(2)]
        hT = [carve(2 * P).rearrange("p (c t) -> p c t", c=2) for q in range(2)]
        yy = [carve(D) for q in range(2)]

        pA = [ps(f"pA{i}", [P, 512]) for i in range(2)]
        pB = [ps(f"pB{i}", [P, 512]) for i in range(2)]
        pT = [ps(f"pT{i}", [P, 512]) for i in range(2)]
        pH = [ps(f"pH{i}", [P, 512]) for i in range(2)]

        front.bank = [pA[0], pA[1]]
        front.stage = [pT[0], pT[1]]
        front.out = [pB[0], pA[1]]
        back.bank = [pH[0], pH[0]]
        back.stage = [pB[1], pH[1]]
        back.out = [pH[1], pH[0]]

        consts_loaded = sem("consts_loaded")
        pool_consts = sem("pool_consts")
        act_consts = sem("act_consts")
        vec = sem("vec")
        x_loaded = sem("x_loaded")
        for v, side in ((front, "f"), (back, "b")):
            v.w_loaded = sem(f"{side}_w_loaded")
            v.var_ready = sem(f"{side}_var_ready")
            v.rstd_ready = sem(f"{side}_rstd_ready")
            v.nmr_ready = sem(f"{side}_nmr_ready")
            v.x_ready = sem(f"{side}_x_ready")
            v.cmax_ready = sem(f"{side}_cmax_ready")
            v.cmaxT_ready = sem(f"{side}_cmaxT_ready")
            v.ratio_ready = sem(f"{side}_ratio_ready")
            v.root_ready = sem(f"{side}_root_ready")
            v.s_ready = sem(f"{side}_s_ready")
            v.bcast_ready = sem(f"{side}_bcast_ready")
            v.s_row_ready = sem(f"{side}_s_row_ready")
            v.w_scaled = sem(f"{side}_w_scaled")
            v.scaled_ready = sem(f"{side}_scaled_ready")
            v.wscale_ready = sem(f"{side}_wscale_ready")
            v.wscale_copied = sem(f"{side}_wscale_copied")
            v.is_rounded = sem(f"{side}_is_rounded")
            v.staged = sem(f"{side}_staged")
            v.unstaged = sem(f"{side}_unstaged")
            v.product = sem(f"{side}_product")
            v.product_used = sem(f"{side}_product_used")
        silu_ready = sem("silu_ready")
        x2_ready = sem("x2_ready")
        x2n_ready = sem("x2n_ready")
        logits_ready = sem("logits_ready")
        logits_copied = sem("logits_copied")
        shifted = sem("shifted")
        exp_ready = sem("exp_ready")
        comb_ready = sem("comb_ready")
        x2_stored = sem("x2_stored")
        x2n_stored = sem("x2n_stored")
        comb_stored = sem("comb_stored")
        member_ready = sem("member_ready")
        ranks_ready = sem("ranks_ready")
        eid_ready = sem("eid_ready")
        eidT_ready = sem("eidT_ready")
        plan_ready = sem("plan_ready")
        slots_ready = sem("slots_ready")
        lo_copied = sem("lo_copied")
        far_ready = sem("far_ready")
        pool_hots = sem("pool_hots")
        act_hots = sem("act_hots")
        dve_hots = sem("dve_hots")
        hot_used = sem("hot_used")
        tab_ready = sem("tab_ready")
        tok_ready = sem("tok_ready")
        w_landed = [sem(f"w_landed{r}") for r in range(RING)]
        weights_ready = sem("weights_ready")
        passed = sem("passed")
        out_idx_ready = sem("out_idx_ready")
        idx_ready = sem("idx_ready")
        gathered = [sem(f"gathered{q}") for q in range(2)]
        gT_filled = sem("gT_filled")
        gT_ready = sem("gT_ready")
        gu_ready = sem("gu_ready")
        gs_ready = sem("gs_ready")
        hh_ready = sem("hh_ready")
        wt_ready = sem("wt_ready")
        hT_filled = sem("hT_filled")
        hT_ready = sem("hT_ready")
        y_filled = sem("y_filled")
        y_ready = sem("y_ready")
        added = [sem(f"added{q}") for q in range(2)]
        additions = sem("additions")

        def x_rows(b, t):
            return x_in[:, bass.ds(b, 1), t, :].rearrange("p a d -> p (a d)")

        block = ctx.enter_context(nc.Block())

        @block.sync
        def _(sp):
            sp.dma_start(gwT[:], gate_w.rearrange("(c p) e -> p c e", p=P)).then_inc(consts_loaded, 16)
            sp.dma_start(gates[:, 0:1], g_x).then_inc(consts_loaded, 16)
            sp.dma_start(gates[:, 1:2], g_f).then_inc(consts_loaded, 16)

            def load_x(b):
                if b > 0:
                    sp.wait_ge(x_loaded, 16 * b)
                sp.dma_start(x_in[:, b], x[b].rearrange("(t p) d -> p t d", p=P)).then_inc(x_loaded, 16)

            def load_w(v, b):
                src = w1 if v is front else w2
                sp.dma_start(v.w_in[:], src[bass.ds(b, 1)].rearrange("a (t p) d -> p (a t) d", p=P)).then_inc(v.w_loaded, 16)

            def next_w(v, b):
                sp.wait_ge(v.w_scaled, DC * b + DC)
                load_w(v, b + 1)

            def store_x2(b):
                sp.wait_ge(x2_ready, TT * b + TT)
                sp.sem_inc(passed, 1)
                sp.dma_start(out[bass.ds(b * T, T), :].rearrange("(t p) d -> p t d", p=P),
                             back.prod[:]).then_inc(x2_stored, 16)

            def store_rows(b):
                sp.wait_ge(x2n_ready, TT * b + TT)
                sp.dma_start(rows[bass.ds(b * T, T), 0:D].rearrange("(t p) d -> p t d", p=P), x2n[:]).then_inc(x2n_stored, 16)
                sp.wait_ge(comb_ready, b + 1)
                sp.dma_start(rows[bass.ds(b * T, T), D:ROW].rearrange("(t p) d -> p t d", p=P), comb[:]).then_inc(comb_stored, 16)

            def load_expert(e, r):
                sp.dma_start(wgu[:, r], gate_up_t[bass.ds(e, 1)].rearrange("a (c p) n -> p (a c) n", p=P)).then_inc(w_landed[r], 16)
                sp.dma_start(wd[:, r, 0, :], down_t[bass.ds(e, 1), 0:P, :].rearrange("a p n -> p (a n)")).then_inc(w_landed[r], 16)
                sp.dma_start(wd[0:FREST, r, 1, :], down_t[bass.ds(e, 1), P:F, :].rearrange("a p n -> p (a n)")).then_inc(w_landed[r], 16)

            load_x(0)
            load_w(front, 0)
            load_x(1)
            load_w(back, 0)
            next_w(front, 0)
            for b in range(2, B):
                load_x(b)
            for r in range(RING):
                load_expert(r, r)
            with sp.Fori(0, B - 2) as b:
                next_w(back, b)
                next_w(front, b + 1)
                store_x2(b)
                store_rows(b)
            next_w(back, B - 2)
            for b in (B - 2, B - 1):
                store_x2(b)
                store_rows(b)

            def announce(r, times):
                sp.wait_ge(w_landed[r], 48 * times)
                sp.sem_inc(weights_ready, 1)

            for r in range(RING - 1):
                announce(r, 1)
            sp.wait_ge(plan_ready, 1)
            with sp.Fori(0, E // RING - 1) as it:
                for r in range(RING):
                    e = it * RING + r
                    last = nc.sync.value_load(tend_i[0:1, bass.ds(e, 1)], min_val=1, max_val=TILES)
                    sp.wait_ge(y_filled, last + 2)
                    load_expert(e + RING, r)
                    announce((r - 1) % RING, it + (1 if r == 0 else 2))
            announce(RING - 1, E // RING)
            sp.wait_ge(x2_stored, 16 + 16 * B)
            sp.wait_ge(x2n_stored, 16 + 16 * B)
            sp.wait_ge(comb_stored, 16 + 16 * B)

        @block.gpsimd
        def _(pool):
            pool.memset(zrow[:], 0.0).then_inc(pool_consts, 1)
            pool.memset(half[:], 0.5).then_inc(pool_consts, 1)
            pool.memset(neghalf[:], -0.5).then_inc(pool_consts, 1)
            pool.memset(magic[:], MAGIC).then_inc(pool_consts, 1)
            pool.memset(nmagic[:], -MAGIC).then_inc(pool_consts, 1)
            pool.memset(ones[:], 1.0).then_inc(pool_consts, 1)
            pool.memset(one_e[:], 1.0).then_inc(pool_consts, 1)
            pool.memset(ident[:], 0.0).then_inc(pool_consts, 1)
            pool.memset(carry[:], 1.0).then_inc(pool_consts, 1)
            pool.iota(iota_e[:], [[1, E]], base=0, channel_multiplier=0,
                      allow_small_or_imprecise_dtypes=True).then_inc(pool_consts, 1)
            pool.iota(iota_lo[:], [[1, P]], base=0, channel_multiplier=0,
                      allow_small_or_imprecise_dtypes=True).then_inc(pool_consts, 1)
            pool.iota(iota_hi[:], [[1, TILES]], base=0, channel_multiplier=0,
                      allow_small_or_imprecise_dtypes=True).then_inc(pool_consts, 1)
            pool.iota(pidx[:], [[P, 2]], base=0, channel_multiplier=1,
                      allow_small_or_imprecise_dtypes=True).then_inc(pool_consts, 1)
            pool.iota(label[:], [[-P, NK]], base=N, channel_multiplier=-1,
                      allow_small_or_imprecise_dtypes=True).then_inc(pool_consts, 1)
            pool.iota(nlabel[:], [[P, NK]], base=-N, channel_multiplier=1,
                      allow_small_or_imprecise_dtypes=True).then_inc(pool_consts, 1)
            pool.wait_ge(pool_consts, 15)
            pool.affine_select(out=ident[:], in_=ident[:], compare_op=ALU.not_equal, fill=1.0,
                               base=0, pattern=[[-1, P]], channel_multiplier=1).then_inc(pool_consts, 1)
            pool.affine_select(out=tri[:], in_=ones[:], compare_op=ALU.is_gt, fill=0.0,
                               base=0, pattern=[[1, P]], channel_multiplier=-1).then_inc(pool_consts, 1)
            pool.affine_select(out=carry[:], in_=carry[:], compare_op=ALU.not_equal, fill=0.0,
                               base=0, pattern=[[0, TT], [1, TOP_K]], channel_multiplier=0).then_inc(pool_consts, 1)

            pool.dma_start(rows[N:N + P, :], zrow[:]).then_inc(added[0], 16)
            pool.dma_start(out[N:N + P, :], zrow[:, 0:D]).then_inc(added[1], 16)

            def inverse_std(v, b):
                pool.wait_ge(v.var_ready, b + 1)
                pool.tensor_tensor(v.rstd[:], v.veps[:], neghalf[:, 0:TT], ALU.pow).then_inc(v.rstd_ready, 1)

            def square_root(v, b):
                pool.wait_ge(v.ratio_ready, b + 1)
                pool.tensor_tensor(v.root[:], v.ratio[:], half[:, 0:v.chunks], ALU.pow).then_inc(v.root_ready, 1)

            def scale_weights(v, b):
                pool.wait_ge(v.s_row_ready, b + 1)
                for t in range(DC):
                    pool.tensor_tensor(v.grid[:, 1, t, :], v.w_in[:, t, :], v.s_row[:], ALU.mult).then_inc(v.w_scaled, 1)

            def gate_times_up(b):
                for t in range(TT):
                    pool.wait_ge(silu_ready, TT * b + t + 1)
                    pool.tensor_tensor(back.grid[:, 0, t, :], sg[:, t, :], front.prod[:, t, I:2 * I], ALU.mult).then_inc(back.x_ready, 1)

            def residual(b):
                for t in range(TT):
                    pool.wait_ge(back.product_used, TT * b + t + 3)
                    pool.tensor_tensor(back.prod[:, t, :], back.prod[:, t, :], x_rows(b, t), ALU.add).then_inc(x2_ready, 1)

            def normalise_second(b):
                pool.wait_ge(back.nmr_ready, b + 1)
                pool.wait_ge(x2n_stored, 16 * b + 16)
                pool.sem_inc(passed, 1)
                for t in range(TT):
                    pool.tensor_scalar(x2n[:, t, :], back.prod[:, t, :], back.rstd[:, t:t + 1], back.nmr[:, t:t + 1],
                                       ALU.mult, ALU.add).then_inc(x2n_ready, 1)

            def entries(b, last):
                residual(b)
                if not last:
                    inverse_std(front, b + 2)
                inverse_std(back, b)
                normalise_second(b)
                gate_times_up(b + 1)
                if not last:
                    square_root(front, b + 2)
                square_root(back, b + 1)
                scale_weights(back, b + 1)
                if not last:
                    scale_weights(front, b + 2)

            inverse_std(front, 0)
            square_root(front, 0)
            scale_weights(front, 0)
            inverse_std(front, 1)
            gate_times_up(0)
            square_root(front, 1)
            square_root(back, 0)
            scale_weights(back, 0)
            scale_weights(front, 1)
            with pool.Fori(0, B - 2) as b:
                entries(b, False)
            entries(B - 2, True)
            residual(B - 1)
            inverse_std(back, B - 1)

            pool.wait_ge(slots_ready, 2)
            with pool.Fori(0, NK) as k:
                pool.wait_ge(pool_hots, len(LO_BY_POOL) * k)
                pool.sem_inc(passed, 1)
                pool.tensor_copy(lo_now[:], lo_f[:, bass.ds(TOP_K * k, TOP_K)]).then_inc(lo_copied, 1)
                pool.wait_ge(lo_copied, k + 1)
                for j in LO_BY_POOL:
                    pool.wait_ge(hot_used, TOP_K * k + j + 1)
                    pool.sem_inc(passed, 1)
                    pool.tensor_scalar(oh_lo[:, j % OH, :], iota_lo[:], lo_now[:, j:j + 1], None, ALU.is_equal).then_inc(pool_hots, 1)

            pool.wait_ge(tok_ready, 1)
            pool.wait_ge(x2_stored, 16 + 16 * B)
            pool.wait_ge(x2n_stored, 16 + 16 * B)
            pool.wait_ge(comb_stored, 16 + 16 * B)
            pool.wait_ge(added[0], 16)
            pool.wait_ge(added[1], 16)

            def gather(i, q):
                pool.tensor_copy(tok_now[q][:, 0:1], tok_i[:, bass.ds(i, 1)]).then_inc(idx_ready, 1)
                pool.wait_ge(idx_ready, i + 1)
                pool.sem_inc(passed, 1)
                pool.indirect_dma_start(out=got[q][:], out_offset=None, in_=rows,
                                        in_offset=bass.IndirectOffsetOnAxis(ap=tok_now[q][:, 0:1], axis=0)
                                        ).then_inc(gathered[q], 16)

            def add_rows(i, q, before):
                pool.wait_ge(added[1 - q], before)
                pool.sem_inc(additions, 1)
                pool.tensor_copy(tok_out[q][:, 0:1], tok_i[:, bass.ds(i, 1)]).then_inc(out_idx_ready, 1)
                pool.wait_ge(out_idx_ready, i + 1)
                pool.wait_ge(y_ready, i + 3)
                pool.sem_inc(passed, 1)
                pool.indirect_dma_start(out=out, out_offset=bass.IndirectOffsetOnAxis(ap=tok_out[q][:, 0:1], axis=0),
                                        in_=yy[q], in_offset=None, compute_op=ALU.add
                                        ).then_inc(added[q], 16)

            pool.sem_inc(additions, 1)
            gather(0, 0)
            gather(1, 1)
            for i in range(2):
                pool.wait_ge(gT_filled, i + 1)
                pool.wait_ge(wt_ready, i + 1)
                gather(i + 2, i)
            trips = nc.gpsimd.value_load(trips_i[0:1, 0:1], min_val=1, max_val=TILES // 2)
            with pool.Fori(0, trips) as it:
                for q in range(2):
                    i = 2 * it + q
                    pool.wait_ge(gT_filled, i + 3)
                    pool.wait_ge(wt_ready, i + 3)
                    gather(i + 4, q)
                    add_rows(i, q, 16 * it + 16 * (q + 1))
            pool.wait_ge(added[0], 16 * trips + 16)
            pool.wait_ge(added[1], 16 * trips + 16)
            pool.wait_ge(gathered[0], 16 * trips + 32)
            pool.wait_ge(gathered[1], 16 * trips + 32)

        @block.scalar
        def _(act_e):
            act_e.sem_inc(front.unstaged, 2)
            act_e.sem_inc(back.unstaged, 2)
            act_e.sem_inc(y_ready, 2)
            act_e.wait_ge(consts_loaded, 48)
            nc.scalar.activation(tg[:], gates[:], ACT.Tanh).then_inc(act_consts, 1)
            act_e.wait_ge(act_consts, 1)
            act_e.wait_ge(pool_consts, 5)

            def normalise(v, b):
                act_e.wait_ge(v.nmr_ready, b + 1)
                if v is back:
                    act_e.wait_ge(x2n_stored, 16 * b + 16)
                for t in range(TT):
                    if v is front:
                        nc.scalar.activation(front.grid[:, 0, t, :], x_rows(b, t),
                                             ACT.Identity, bias=v.nmr[:, t:t + 1], scale=v.rstd[:, t:t + 1]).then_inc(front.x_ready, 1)
                    else:
                        nc.scalar.activation(x2n[:, t, :], back.prod[:, t, :], ACT.Identity, bias=v.nmr[:, t:t + 1],
                                             scale=v.rstd[:, t:t + 1]).then_inc(x2n_ready, 1)

            def copy_s(v, b):
                act_e.wait_ge(v.bcast_ready, b + 1)
                lo = 0 if v is front else I
                nc.scalar.activation(v.s_row[:], v.bank[1][:, lo:lo + v.width], ACT.Copy).then_inc(v.s_row_ready, 1)

            def round_rows(v, b):
                act_e.wait_ge(v.scaled_ready, b + 1)
                for g in range(2):
                    for t in range(TT):
                        nc.scalar.activation(v.grid[:, g, t, :], v.grid[:, g, t, :], ACT.Identity,
                                             bias=magic[:, 0:1], scale=v.rq[:, g, t:t + 1]).then_inc(v.is_rounded, 1)

            def copy_wscale(v, b):
                act_e.wait_ge(v.wscale_ready, b + 1)
                if v is front:
                    nc.scalar.activation(v.wscale[:], v.bank[0][:], ACT.Copy).then_inc(v.wscale_copied, 1)
                else:
                    nc.scalar.activation(v.wscale[:], v.stage[1][:], ACT.Copy, scale=tg[:, 0:1]).then_inc(v.wscale_copied, 1)

            def unstage(v, b):
                for g in range(2):
                    for c in range(v.chunks):
                        k = g * v.chunks + c
                        act_e.wait_ge(v.staged, 8 * b + k + 1)
                        nc.scalar.activation(v.qT[:, g, c, :], v.stage[k % 2][:], ACT.Identity,
                                             bias=nmagic[:, 0:1], scale=1.0).then_inc(v.unstaged, 1)

            def tokens_across(b):
                for t in range(TT):
                    k = 2 * IC + t
                    act_e.wait_ge(back.staged, 8 * b + k + 1)
                    nc.scalar.activation(x2nT[:, t], back.stage[k % 2][:].rearrange("p (c t) -> p c t", c=DC), ACT.Copy).then_inc(back.unstaged, 1)
                act_e.wait_ge(logits_ready, b + 1)
                nc.scalar.activation(L[:], front.out[0][:, 0:TT * E].rearrange("p (t e) -> p t e", e=E), ACT.Copy).then_inc(logits_copied, 1)

            def silu_gate_half(b):
                for t in range(TT):
                    act_e.wait_ge(front.product_used, TT * b + t + 3)
                    nc.scalar.activation(sg[:, t, :], front.prod[:, t, 0:I], ACT.Silu).then_inc(silu_ready, 1)

            def exponentials(b):
                act_e.wait_ge(shifted, b + 1)
                nc.scalar.activation(eL[:], Lc[:], ACT.Exp).then_inc(exp_ready, 1)
                nc.scalar.activation(tv[:], topc[:], ACT.Exp).then_inc(exp_ready, 1)

            normalise(front, 0)
            copy_s(front, 0)
            round_rows(front, 0)
            copy_wscale(front, 0)
            unstage(front, 0)
            normalise(front, 1)
            silu_gate_half(0)
            copy_s(back, 0)
            copy_s(front, 1)

            def entries(b, last):
                round_rows(back, b)
                copy_wscale(back, b)
                unstage(back, b)
                round_rows(front, b + 1)
                copy_wscale(front, b + 1)
                unstage(front, b + 1)
                if not last:
                    normalise(front, b + 2)
                silu_gate_half(b + 1)
                tokens_across(b)
                exponentials(b)
                copy_s(back, b + 1)
                if not last:
                    copy_s(front, b + 2)

            with act_e.Fori(0, B - 2) as b:
                entries(b, False)
            entries(B - 2, True)
            round_rows(back, B - 1)
            copy_wscale(back, B - 1)
            unstage(back, B - 1)
            normalise(back, B - 1)
            tokens_across(B - 1)
            exponentials(B - 1)

            act_e.wait_ge(slots_ready, 2)
            with act_e.Fori(0, NK) as k:
                act_e.wait_ge(act_hots, len(HI_BY_ACT) * k)
                act_e.sem_inc(passed, 1)
                for a, j in enumerate(HI_BY_ACT):
                    nc.scalar.activation(far[:, a, :], iota_hi[:], ACT.Abs, bias=hi_f[:, bass.ds(TOP_K * k + j, 1)], scale=-1.0).then_inc(far_ready, 1)
                for a, j in enumerate(HI_BY_ACT):
                    act_e.wait_ge(far_ready, len(HI_BY_ACT) * k + a + 1)
                    act_e.wait_ge(hot_used, TOP_K * k + j + 1)
                    act_e.sem_inc(passed, 1)
                    nc.scalar.activation(oh_hi[:, j % OH, :], far[:, a, :], ACT.Relu, bias=label[:, bass.ds(k, 1)],
                                         scale=nlabel[:, bass.ds(k, 1)]).then_inc(act_hots, 1)

            act_e.wait_ge(tok_ready, 1)

            def rows_across(i, q):
                act_e.wait_ge(gT_filled, i + 1)
                nc.scalar.activation(gT[q], pT[q][:].rearrange("p (c t) -> p c t", c=DC), ACT.Copy).then_inc(gT_ready, 1)

            def silu_gate(i, q):
                act_e.wait_ge(gu_ready, i + 1)
                nc.scalar.activation(gs[q], pH[q][:, 0:F], ACT.Silu).then_inc(gs_ready, 1)

            def weigh_rows(i, q):
                act_e.wait_ge(y_filled, i + 3)
                act_e.wait_ge(additions, i + 1)
                nc.scalar.activation(yy[q], pB[q][:], ACT.Copy, scale=wt[:, bass.ds(i, 1)]).then_inc(y_ready, 1)

            trips = nc.scalar.value_load(trips_i[0:1, 0:1], min_val=1, max_val=TILES // 2)
            rows_across(0, 0)
            rows_across(1, 1)
            silu_gate(0, 0)
            with act_e.Fori(0, trips) as it:
                for i, q in ((2 * it + 1, 1), (2 * it + 2, 0)):
                    rows_across(i + 1, 1 - q)
                    silu_gate(i, q)
                    act_e.wait_ge(wt_ready, i)
                    weigh_rows(i - 1, 1 - q)

        @block.tensor
        def _(pe):
            pe.wait_ge(pool_consts, 18)
            pe.wait_ge(consts_loaded, 48)
            pe.sem_inc(y_filled, 2)

            def column_maxima(v, b):
                pe.wait_ge(v.cmax_ready, 2 * b + 2)
                for g in range(2):
                    for c in range(v.chunks):
                        at = (c if v is front else g * v.chunks + c) * P
                        mm = nc.tensor.transpose(v.bank[g][:, at:at + P], v.cmax[:, g, c * P:(c + 1) * P], ident[:])
                mm.then_inc(v.cmaxT_ready, 1)

            def spread(dst, col):
                return nc.tensor.matmul(dst, col.to_broadcast([P, P]), ident[:], start=True, stop=True)

            def column_scales(v, b):
                pe.wait_ge(v.s_ready, b + 1)
                for g in range(2):
                    for c in range(v.chunks):
                        at = (c if v is front else g * v.chunks + c) * P
                        mm = spread(v.bank[g][:, at:at + P], v.sv[:, g, c:c + 1])
                mm.then_inc(v.bcast_ready, 1)

            def weight_scales(v, b):
                pe.wait_ge(v.scaled_ready, b + 1)
                dst = v.bank[0] if v is front else v.stage[1]
                for t in range(DC):
                    mm = spread(dst[:, t * P:(t + 1) * P], v.rscale[:, 1, t:t + 1])
                mm.then_inc(v.wscale_ready, 1)

            def stage_columns(v, b):
                for g in range(2):
                    for c in range(v.chunks):
                        k = g * v.chunks + c
                        pe.wait_ge(v.unstaged, 8 * b + k + 1)
                        if v is back and k == 1:
                            pe.wait_ge(back.wscale_copied, b + 1)
                        for t in range(TT):
                            if c == 0:
                                pe.wait_ge(v.is_rounded, 8 * b + 4 * g + t + 1)
                            mm = nc.tensor.transpose(v.stage[k % 2][:, t * P:(t + 1) * P],
                                                     v.grid[:, g, t, c * P:(c + 1) * P], ident[:])
                        mm.then_inc(v.staged, 1)

            def products(v, b):
                pe.wait_ge(v.unstaged, 8 * b + 2 * v.chunks + 2)
                if v is front and not (isinstance(b, int) and b == 0):
                    pe.wait_ge(logits_copied, b - 1)
                for t in range(TT):
                    pe.wait_ge(v.product_used, TT * b + t + 1)
                    for c in range(v.chunks):
                        mm = nc.tensor.matmul(v.out[t % 2][:], v.qT[:, 0, c, t * P:(t + 1) * P], v.qT[:, 1, c, :],
                                              start=(c == 0), stop=(c == v.chunks - 1))
                    mm.then_inc(v.product, 1)

            def logits(b):
                def rows_up(t):
                    k = 2 * IC + t
                    pe.wait_ge(x2n_ready, TT * b + t + 1)
                    pe.wait_ge(back.unstaged, 8 * b + k + 1)
                    for c in range(DC):
                        mm = nc.tensor.transpose(back.stage[k % 2][:, c * P:(c + 1) * P], x2n[:, t, c * P:(c + 1) * P], ident[:])
                    mm.then_inc(back.staged, 1)

                rows_up(0)
                for t in range(TT):
                    if t + 1 < TT:
                        rows_up(t + 1)
                    pe.wait_ge(back.unstaged, 8 * b + 2 * IC + t + 3)
                    for c in range(DC):
                        mm = nc.tensor.matmul(front.out[0][:, t * E:(t + 1) * E], x2nT[:, t, c, :], gwT[:, c, :],
                                              start=(c == 0), stop=(c == DC - 1))
                mm.then_inc(logits_ready, 1)

            column_maxima(front, 0)
            column_scales(front, 0)
            weight_scales(front, 0)
            stage_columns(front, 0)
            products(front, 0)
            column_maxima(front, 1)
            column_maxima(back, 0)
            column_scales(back, 0)
            column_scales(front, 1)

            def entries(b, last):
                weight_scales(back, b)
                stage_columns(back, b)
                products(back, b)
                weight_scales(front, b + 1)
                stage_columns(front, b + 1)
                products(front, b + 1)
                logits(b)
                if not last:
                    column_maxima(front, b + 2)
                column_maxima(back, b + 1)
                column_scales(back, b + 1)
                if not last:
                    column_scales(front, b + 2)

            with pe.Fori(0, B - 2) as b:
                entries(b, False)
            entries(B - 2, True)
            weight_scales(back, B - 1)
            stage_columns(back, B - 1)
            products(back, B - 1)
            logits(B - 1)

            pe.wait_ge(comb_ready, B)
            mflat = member[:].rearrange("p k e -> p (k e)")
            nc.tensor.matmul(pA[0][:], tri[:], mflat, start=True, stop=True)
            nc.tensor.matmul(pA[1][:], ones[:], mflat, start=True, stop=True).then_inc(ranks_ready, 1)
            pe.wait_ge(eid_ready, 1)
            for g in range(2):
                mm = spread(pB[0][:, g * P:(g + 1) * P], eid_c[:, g:g + 1])
            mm.then_inc(eidT_ready, 1)
            zero_lo, zero_hi = zrow[:, 0:P // 2].bitcast(FP16), zrow[:, 0:TILES // 2].bitcast(FP16)
            nc.tensor.matmul(pB[1][:, 0:TILES], zero_lo, zero_hi, start=True, stop=False, skip_group_check=True)
            with pe.Fori(0, NK) as k:
                for j in range(TOP_K):
                    made = 2 * (j + 1)
                    if j in LO_BY_POOL:
                        pe.wait_ge(pool_hots, len(LO_BY_POOL) * k + LO_BY_POOL.index(j) + 1)
                    if j in HI_BY_ACT:
                        pe.wait_ge(act_hots, len(HI_BY_ACT) * k + HI_BY_ACT.index(j) + 1)
                    if not (j in LO_BY_POOL and j in HI_BY_ACT):
                        made -= sum(c <= j for c in LO_BY_POOL) + sum(c <= j for c in HI_BY_ACT)
                        pe.wait_ge(dve_hots, (2 * TOP_K - len(LO_BY_POOL) - len(HI_BY_ACT)) * k + made)
                    nc.tensor.matmul(pB[1][:, 0:TILES], oh_lo[:, j % OH, :], oh_hi[:, j % OH, :],
                                     start=False, stop=False, skip_group_check=True).then_inc(hot_used, 1)
            nc.tensor.matmul(pB[1][:, 0:TILES], zero_lo, zero_hi, start=False, stop=True,
                             skip_group_check=True).then_inc(tab_ready, 1)

            pe.wait_ge(tok_ready, 1)

            def rows_across(i, q):
                if q == 0:
                    pe.wait_ge(gathered[0], 8 * i + 16)
                else:
                    pe.wait_ge(gathered[1], 8 * i + 8)
                for c in range(DC):
                    mm = nc.tensor.transpose(pT[q][:, c * P:(c + 1) * P], got[q][:, c * P:(c + 1) * P], ident[:])
                mm.then_inc(gT_filled, 1)

            def gate_up(i, q):
                e = nc.tensor.value_load(eid_i[0:1, bass.ds(i, 1)], min_val=0, max_val=E - 1)
                slot = nc.tensor.snap(e % RING, min_val=0, max_val=RING - 1)
                pe.wait_ge(weights_ready, e + 1)
                pe.wait_ge(gT_ready, i + 1)
                for c in range(DC):
                    mm = nc.tensor.matmul(pH[q][:, 0:GU], gT[q][:, c, :], wgu[:, bass.ds(slot, 1), c, :],
                                          start=(c == 0), stop=(c == DC - 1))
                mm.then_inc(gu_ready, 1)

            def inner_across(i, q):
                pe.wait_ge(hh_ready, i + 1)
                nc.tensor.transpose(pA[q][:, 0:P], hh[q][:, 0:P], ident[:])
                nc.tensor.transpose(pA[q][0:FREST, P:2 * P], hh[q][:, P:F], ident[:]).then_inc(hT_filled, 1)

            def down(i, q):
                e = nc.tensor.value_load(eid_i[0:1, bass.ds(i, 1)], min_val=0, max_val=E - 1)
                slot = nc.tensor.snap(e % RING, min_val=0, max_val=RING - 1)
                pe.wait_ge(hT_ready, i + 1)
                pe.wait_ge(y_ready, i + 1)
                nc.tensor.matmul(pB[q][:], hT[q][:, 0, :], wd[:, bass.ds(slot, 1), 0, :], start=True, stop=False)
                nc.tensor.matmul(pB[q][:], hT[q][0:FREST, 1, :], wd[0:FREST, bass.ds(slot, 1), 1, :],
                                 start=False, stop=True).then_inc(y_filled, 1)

            trips = nc.tensor.value_load(trips_i[0:1, 0:1], min_val=1, max_val=TILES // 2)
            rows_across(0, 0)
            rows_across(1, 1)
            gate_up(0, 0)
            with pe.Fori(0, trips) as it:
                for i, q in ((2 * it + 1, 1), (2 * it + 2, 0)):
                    pe.wait_ge(gT_ready, i)
                    rows_across(i + 1, 1 - q)
                    inner_across(i - 1, 1 - q)
                    gate_up(i, q)
                    down(i - 1, 1 - q)

        @block.vector
        def _(dve):
            count = [0, 0]

            def step(ins):
                count[0] += 1
                return ins.then_inc(vec, 1)

            def settle():
                dve.wait_ge(vec, count[1] + count[0])

            dve.sem_inc(front.product_used, 2)
            dve.sem_inc(back.product_used, 2)
            dve.sem_inc(hot_used, OH)
            dve.sem_inc(x2_stored, 16)
            dve.sem_inc(x2n_stored, 16)
            dve.sem_inc(comb_stored, 16)
            dve.wait_ge(pool_consts, 18)

            def statistics(v, b):
                if v is front:
                    dve.wait_ge(x_loaded, 16 * b + 16)
                for t in range(TT):
                    if v is back:
                        dve.wait_ge(x2_ready, TT * b + t + 1)
                    step(nc.vector.bn_stats(v.bn[:, t, :], back.prod[:, t, :] if v is back else x_rows(b, t)))
                settle()
                dve.sem_inc(passed, 1)
                for t in range(TT):
                    step(nc.vector.bn_aggr(v.mv[:, t, :], v.bn[:, t, :]))
                settle()
                nc.vector.tensor_scalar(v.veps[:], v.mv[:, :, 1], EPS_LN, None, ALU.add).then_inc(v.var_ready, 1)

            def mean_over_std(v, b):
                dve.wait_ge(v.rstd_ready, b + 1)
                nc.vector.scalar_tensor_tensor(out=v.nmr[:], in0=v.mv[:, :, 0], scalar=-1.0, in1=v.rstd[:],
                                               op0=ALU.mult, op1=ALU.mult).then_inc(v.nmr_ready, 1)

            def weight_maxima(v, b):
                dve.wait_ge(v.w_loaded, 16 * b + 16)
                nc.vector.tensor_reduce(v.cmax[:, 1, :], v.w_in[:].rearrange("p t d -> p d t"), AX.X, ALU.max,
                                        apply_absolute_value=True).then_inc(v.cmax_ready, 1)

            def activation_maxima(v, b):
                dve.wait_ge(v.x_ready, TT * b + TT)
                nc.vector.tensor_reduce(v.cmax[:, 0, :], v.grid[:, 0].rearrange("p t d -> p d t"), AX.X, ALU.max,
                                        apply_absolute_value=True).then_inc(v.cmax_ready, 1)

            def column_ratio(v, b):
                dve.wait_ge(v.cmaxT_ready, b + 1)
                if v is front:
                    for g in range(2):
                        step(nc.vector.tensor_reduce(v.am[:, g, :], v.bank[g][:].rearrange("p (c t) -> p c t", t=P), AX.X, ALU.max))
                else:
                    step(nc.vector.tensor_reduce(v.am[:].rearrange("p g c -> p (g c)"), v.bank[0][:].rearrange("p (c t) -> p c t", t=P),
                                                 AX.X, ALU.max))
                settle()
                step(nc.vector.tensor_scalar(v.am[:], v.am[:], EPS_Q, None, ALU.max))
                settle()
                step(nc.vector.reciprocal(v.ramw[:], v.am[:, 1, :]))
                settle()
                nc.vector.tensor_tensor(v.ratio[:], v.am[:, 0, :], v.ramw[:], ALU.mult).then_inc(v.ratio_ready, 1)

            def column_scale(v, b):
                dve.wait_ge(v.root_ready, b + 1)
                step(nc.vector.reciprocal(v.rroot[:], v.root[:]))
                settle()
                step(nc.vector.tensor_tensor(v.rroot[:], v.ratio[:], v.rroot[:], ALU.mult))
                settle()
                step(nc.vector.tensor_tensor(v.rroot[:], v.root[:], v.rroot[:], ALU.add))
                settle()
                step(nc.vector.tensor_scalar(v.sv[:, 1, :], v.rroot[:], 0.5, EPS_Q, ALU.mult, ALU.max))
                settle()
                nc.vector.reciprocal(v.sv[:, 0, :], v.sv[:, 1, :]).then_inc(v.s_ready, 1)

            def scale_x(v, b):
                dve.wait_ge(v.bcast_ready, b + 1)
                if v is back:
                    dve.wait_ge(back.s_row_ready, b + 1)
                step(nc.vector.tensor_tensor(v.grid[:, 0], v.grid[:, 0],
                                             v.bank[0][:, 0:v.width].unsqueeze(1).to_broadcast([P, TT, v.width]), ALU.mult))

            def row_scales(v, b):
                settle()
                step(nc.vector.tensor_reduce(v.rmax[:, 0, :], v.grid[:, 0], AX.X, ALU.max, apply_absolute_value=True))
                dve.wait_ge(v.w_scaled, DC * b + DC)
                step(nc.vector.tensor_reduce(v.rmax[:, 1, :], v.grid[:, 1], AX.X, ALU.max, apply_absolute_value=True))
                settle()
                step(nc.vector.tensor_scalar(v.rscale[:], v.rmax[:], EPS_Q, 1.0 / QMAX, ALU.max, ALU.mult))
                settle()
                nc.vector.reciprocal(v.rq[:], v.rscale[:]).then_inc(v.scaled_ready, 1)

            def dequantise(v, b):
                dve.wait_ge(v.wscale_copied, b + 1)
                if v is back:
                    dve.wait_ge(x2_stored, 16 * b + 16)
                    dve.wait_ge(x2n_stored, 16 * b + 16)
                for t in range(TT):
                    dve.wait_ge(v.product, TT * b + t + 1)
                    nc.vector.scalar_tensor_tensor(out=v.prod[:, t, :], in0=v.out[t % 2][:], scalar=v.rscale[:, 0, t:t + 1],
                                                   in1=v.wscale[:], op0=ALU.mult, op1=ALU.mult).then_inc(v.product_used, 1)

            def choose(b):
                k0 = TT * b
                dve.wait_ge(logits_copied, b + 1)
                dve.sem_inc(passed, 1)
                for t in range(TT):
                    step(nc.vector.max(top[:, t, :], L[:, t, :]))
                settle()
                dve.sem_inc(passed, 1)
                for t in range(TT):
                    step(nc.vector.max_index(idx[:, t, :], top[:, t, :], L[:, t, :]))
                first = top[:, :, 0:1]
                step(nc.vector.tensor_tensor(Lc[:], L[:], first.to_broadcast([P, TT, E]), ALU.subtract))
                nc.vector.tensor_tensor(topc[:], top[:], first.to_broadcast([P, TT, TOP_K]), ALU.subtract).then_inc(shifted, 1)
                settle()
                step(nc.vector.tensor_copy(idxf[:], idx[:]))
                settle()
                step(nc.vector.tensor_tensor(
                    onehot[:, bass.ds(k0, TT), :, :],
                    iota_e[:].unsqueeze(1).unsqueeze(1).to_broadcast([P, TT, TOP_K, E]),
                    idxf[:].unsqueeze(3).to_broadcast([P, TT, TOP_K, E]), ALU.is_equal))

            def combine(b):
                k0 = TT * b
                dve.wait_ge(exp_ready, 2 * b + 2)
                step(nc.vector.tensor_reduce(sumL[:], eL[:], AX.X, ALU.add))
                settle()
                step(nc.vector.reciprocal(rsumL[:], sumL[:]))
                settle()
                step(nc.vector.tensor_tensor(tv[:], tv[:], rsumL[:].unsqueeze(2).to_broadcast([P, TT, TOP_K]), ALU.mult))
                settle()

                def normalised(dst, src):
                    step(nc.vector.tensor_reduce(ssum[:], src, AX.X, ALU.add))
                    settle()
                    step(nc.vector.tensor_scalar(ssum[:], ssum[:], SUM_FLOOR, None, ALU.max))
                    settle()
                    step(nc.vector.reciprocal(rsum[:], ssum[:]))
                    settle()
                    step(nc.vector.tensor_tensor(dst, src, rsum[:].unsqueeze(2).to_broadcast([P, TT, TOP_K]), ALU.mult))
                    settle()

                normalised(ren[:], tv[:])
                step(nc.vector.tensor_tensor_scan(cum[:].rearrange("p t j -> p (t j)"), carry[:].rearrange("p t j -> p (t j)"),
                                                  ren[:].rearrange("p t j -> p (t j)"), 0.0, ALU.mult, ALU.add))
                settle()
                step(nc.vector.tensor_scalar(keep[:, :, 1:TOP_K], cum[:, :, 0:TOP_K - 1], THRESHOLD, None, ALU.is_lt))
                settle()
                step(nc.vector.tensor_tensor(rw[:], tv[:], keep[:], ALU.mult))
                settle()
                normalised(rw[:], rw[:])
                step(nc.vector.tensor_scalar(active[:, bass.ds(k0, TT), :], rw[:], 0.0, None, ALU.is_gt))
                step(nc.vector.tensor_tensor(prod[:], onehot[:, bass.ds(k0, TT), :, :],
                                             rw[:].unsqueeze(3).to_broadcast([P, TT, TOP_K, E]), ALU.mult))
                settle()
                step(nc.vector.tensor_reduce(eL[:], prod[:].rearrange("p t j e -> p t e j"), AX.X, ALU.add))
                settle()
                step(nc.vector.tensor_scalar(member[:, bass.ds(k0, TT), :], eL[:], 0.0, None, ALU.is_gt))
                dve.wait_ge(comb_stored, 16 * b + 16)
                nc.vector.tensor_scalar(comb[:], eL[:], tg[:, 1:2], None, ALU.mult).then_inc(comb_ready, 1)

            dve.wait_ge(act_consts, 1)
            nc.vector.memset(keep[:], 1.0)
            statistics(front, 0)
            weight_maxima(front, 0)
            mean_over_std(front, 0)
            activation_maxima(front, 0)
            column_ratio(front, 0)
            column_scale(front, 0)
            scale_x(front, 0)
            row_scales(front, 0)
            statistics(front, 1)
            mean_over_std(front, 1)
            weight_maxima(front, 1)
            weight_maxima(back, 0)
            dequantise(front, 0)
            activation_maxima(front, 1)
            column_ratio(front, 1)
            activation_maxima(back, 0)
            column_ratio(back, 0)
            column_scale(back, 0)
            column_scale(front, 1)
            scale_x(back, 0)
            row_scales(back, 0)
            scale_x(front, 1)
            row_scales(front, 1)
            before = count[0]

            def entries(b, last):
                count[:] = [0, before + b * STEPS_PER_PASS]
                dequantise(back, b)
                if not last:
                    statistics(front, b + 2)
                statistics(back, b)
                if not last:
                    mean_over_std(front, b + 2)
                mean_over_std(back, b)
                if not last:
                    dequantise(front, b + 1)
                    activation_maxima(front, b + 2)
                    weight_maxima(front, b + 2)
                    weight_maxima(back, b + 1)
                    column_ratio(front, b + 2)
                else:
                    dequantise(front, b + 1)
                    weight_maxima(back, b + 1)
                activation_maxima(back, b + 1)
                column_ratio(back, b + 1)
                column_scale(back, b + 1)
                if not last:
                    column_scale(front, b + 2)
                choose(b)
                scale_x(back, b + 1)
                row_scales(back, b + 1)
                if not last:
                    scale_x(front, b + 2)
                    row_scales(front, b + 2)
                combine(b)
                assert last or count[0] == STEPS_PER_PASS, count

            with dve.Fori(0, B - 2) as b:
                entries(b, False)
            entries(B - 2, True)
            dequantise(back, B - 1)
            statistics(back, B - 1)
            mean_over_std(back, B - 1)
            choose(B - 1)
            combine(B - 1)

            dve.wait_ge(x2_stored, 16 + 16 * B)
            dve.wait_ge(comb_ready, B)
            dve.wait_ge(ranks_ready, 1)
            step(nc.vector.tensor_copy(tot, pA[1][:].rearrange("p (k e) -> p k e", e=E)))
            settle()
            src, d, flip = tot, 1, 0
            while d < NK:
                dst = pre[flip]
                step(nc.vector.tensor_copy(dst[:, 0:d, :], src[:, 0:d, :]))
                step(nc.vector.tensor_tensor(dst[:, d:NK, :], src[:, d:NK, :], src[:, 0:NK - d, :], ALU.add))
                settle()
                src, d, flip = dst, 2 * d, 1 - flip
            step(nc.vector.tensor_scalar(cnt_i[:], src[:, NK - 1, :], float(P - 1), None, ALU.add))
            settle()
            step(nc.vector.tensor_scalar(tend_i[:], cnt_i[:], 7, None, ALU.logical_shift_right))
            settle()
            step(nc.vector.tensor_scalar(tiles_f[:], tend_i[:], 1.0, None, ALU.max))
            settle()
            step(nc.vector.tensor_tensor_scan(tend[:], one_e[:], tiles_f[:], 0.0, ALU.mult, ALU.add))
            settle()
            step(nc.vector.tensor_copy(tend_i[:], tend[:]))
            step(nc.vector.tensor_scalar(cnt_i[:, 0:1], tend[:, E - 1:E], 1.0, None, ALU.add))
            for g in range(2):
                step(nc.vector.tensor_scalar(cmp[:], tend[:], pidx[:, g:g + 1], None, ALU.is_le))
                settle()
                step(nc.vector.tensor_reduce(eid_c[:, g:g + 1], cmp[:], AX.X, ALU.add))
                settle()
            nc.vector.tensor_scalar(eid_c[:], eid_c[:], float(E - 1), None, ALU.min).then_inc(eid_ready, 1)
            step(nc.vector.tensor_scalar(trips_i[:], cnt_i[:, 0:1], 1, None, ALU.logical_shift_right))
            step(nc.vector.tensor_tensor(base_e[:], tend[:], tiles_f[:], ALU.subtract))
            step(nc.vector.tensor_tensor(slot_e, src[:], tot, ALU.subtract))
            settle()
            step(nc.vector.tensor_tensor(slot_e, slot_e, pA[0][:].rearrange("p (k e) -> p k e", e=E), ALU.add))
            settle()
            step(nc.vector.scalar_tensor_tensor(out=slot_e, in0=base_e[:].unsqueeze(1).to_broadcast([P, NK, E]), scalar=float(P),
                                                in1=slot_e, op0=ALU.mult, op1=ALU.add))
            dve.wait_ge(eidT_ready, 1)
            step(nc.vector.tensor_copy(eid_f[:], pB[0][:, 0:2 * P]))
            step(nc.vector.tensor_copy(eid_i[:], pB[0][:, 0:2 * P]))
            settle()
            for k in range(0, NK, TT):
                step(nc.vector.tensor_tensor(prod[:], onehot[:, k:k + TT, :, :],
                                             slot_e[:, k:k + TT, :].unsqueeze(2).to_broadcast([P, TT, TOP_K, E]), ALU.mult))
                settle()
                step(nc.vector.tensor_reduce(slot_f[:, k:k + TT, :], prod[:], AX.X, ALU.add))
                settle()
            step(nc.vector.scalar_tensor_tensor(out=slot_f, in0=active[:], scalar=-32768.0, in1=slot_f,
                                                op0=ALU.mult, op1=ALU.add))
            settle()
            step(nc.vector.tensor_scalar(slot_i, slot_f.rearrange("p k j -> p (k j)"), 32768.0, None, ALU.add))
            settle()
            step(nc.vector.tensor_scalar(lo_i, slot_i, P - 1, None, ALU.bitwise_and))
            step(nc.vector.tensor_scalar(hi_i, slot_i, 7, None, ALU.logical_shift_right))
            settle()
            nc.vector.tensor_copy(lo_f, lo_i).then_inc(slots_ready, 1)
            nc.vector.tensor_copy(hi_f, hi_i).then_inc(slots_ready, 1)
            dve.wait_ge(slots_ready, 2)
            settle()
            with dve.Fori(0, NK) as k:
                for j in range(TOP_K):
                    n = TOP_K * k + j
                    dve.wait_ge(hot_used, n + 1)
                    if j not in LO_BY_POOL:
                        nc.vector.tensor_scalar(oh_lo[:, j % OH, :], iota_lo[:], lo_f[:, bass.ds(n, 1)], None,
                                                ALU.is_equal).then_inc(dve_hots, 1)
                    if j not in HI_BY_ACT:
                        nc.vector.tensor_scalar(oh_hi[:, j % OH, :], iota_hi[:], hi_f[:, bass.ds(n, 1)], label[:, bass.ds(k, 1)],
                                                ALU.is_equal, ALU.mult).then_inc(dve_hots, 1)
            dve.wait_ge(tab_ready, 1)
            step(nc.vector.tensor_scalar(pad[:], pB[1][:, 0:TILES], 0.0, pidx[:, 0:1], ALU.is_equal, ALU.mult))
            step(nc.vector.tensor_scalar(tok_f[:, 0:TILES], pB[1][:, 0:TILES], -1.0, float(N), ALU.mult, ALU.add))
            step(nc.vector.tensor_scalar(tok_i[:, TILES:TABW], one_e[:, 0:TABW - TILES], float(N), pidx[:, 0:1], ALU.mult, ALU.add))
            settle()
            nc.vector.tensor_tensor(tok_i[:, 0:TILES], tok_f[:, 0:TILES], pad[:], ALU.add).then_inc(plan_ready, 1)
            dve.wait_ge(plan_ready, 1)
            dve.sem_inc(tok_ready, 1)

            def row_weights(i, q):
                if q == 0:
                    dve.wait_ge(gathered[0], 8 * i + 16)
                else:
                    dve.wait_ge(gathered[1], 8 * i + 8)
                nc.vector.scalar_tensor_tensor(out=pick[q][:], in0=iota_e[:], scalar=eid_f[:, bass.ds(i, 1)], in1=got[q][:, D:ROW],
                                               op0=ALU.is_equal, op1=ALU.mult,
                                               accum_out=wt[:, bass.ds(i, 1)]).then_inc(wt_ready, 1)

            def inner(i, q):
                dve.wait_ge(gs_ready, i + 1)
                nc.vector.tensor_tensor(hh[q], gs[q], pH[q][:, F:GU], ALU.mult).then_inc(hh_ready, 1)

            def inner_across(i, q):
                dve.wait_ge(hT_filled, i + 1)
                dve.wait_ge(y_filled, i + 1)
                nc.vector.tensor_copy(hT[q], pA[q][:, 0:2 * P].rearrange("p (c t) -> p c t", c=2)).then_inc(hT_ready, 1)

            trips = nc.vector.value_load(trips_i[0:1, 0:1], min_val=1, max_val=TILES // 2)
            row_weights(0, 0)
            row_weights(1, 1)
            inner(0, 0)
            with dve.Fori(0, trips) as it:
                for i, q in ((2 * it + 1, 1), (2 * it + 2, 0)):
                    row_weights(i + 1, 1 - q)
                    inner_across(i - 1, 1 - q)
                    inner(i, q)


_INS = ["x", "fside_BxS2xS2_0", "ctx_1024", "g_xattn", "g_ffn", "L0_ffn_gate_weight", "L0_ffn_gate_up_proj",
        "L0_ffn_down_proj"]


def kernel(**inputs):
    import numpy as _np
    import concourse.bacc as _bacc
    from concourse import mybir as _mybir
    from concourse.bass_utils import run_bass_kernel_spmd as _run

    data = {n: _np.asarray(inputs[n]) for n in _INS}
    B, T, D = data["x"].shape
    for n in ("g_xattn", "g_ffn"):
        data[n] = _np.broadcast_to(data[n].reshape(1, 1), (P, 1))
    data["L0_ffn_gate_weight"] = data["L0_ffn_gate_weight"].T
    data["L0_ffn_gate_up_proj"] = data["L0_ffn_gate_up_proj"].transpose(0, 2, 1)
    data["L0_ffn_down_proj"] = data["L0_ffn_down_proj"].transpose(0, 2, 1)

    nc = _bacc.Bacc("TRN2", target_bir_lowering=False, num_devices=1)
    arrays, args = {}, []
    for name in _INS:
        a = _np.ascontiguousarray(data[name])
        arrays[f"in_{name}"] = a
        args.append(nc.dram_tensor(f"in_{name}", a.shape, _mybir.dt.from_np(a.dtype), kind="ExternalInput").ap())
    args.append(nc.dram_tensor("out_rows", (B * T + P, D), _mybir.dt.from_np(_np.dtype("float32")), kind="ExternalOutput").ap())
    build(nc, *args)
    r = _run(nc, [arrays], core_ids=[0])
    return r.results[0]["out_rows"][0:B * T].reshape(B, T, D)
```

```python
from contextlib import ExitStack

import concourse.bass as bass
from concourse import mybir

P = 128
STEPS_PER_PASS = 68
ALU = mybir.AluOpType
ACT = mybir.ActivationFunctionType
F32 = mybir.dt.float32
F32R = mybir.dt.float32r
BF16 = mybir.dt.bfloat16
FP16 = mybir.dt.float16
I32 = mybir.dt.int32
U32 = mybir.dt.uint32
AX = mybir.AxisListType

EPS_Q = 1e-6
EPS_LN = 1e-5
QMAX = 127.0
MAGIC = 1.5 * 2.0 ** 23
TOP_K = 8
THRESHOLD = 0.8
SUM_FLOOR = 1e-12


class Linear:
    pass


def build(nc, x, w1, w2, g_x, g_f, gate_w, gate_up_t, down_t, out):
    B, T, D = x.shape
    I = w2.shape[2]
    E, _, GU = gate_up_t.shape
    F = GU // 2
    TT = T // P
    DC = D // P
    IC = I // P
    NK = B * TT
    N = B * T
    FREST = F - P
    TILES = N * TOP_K // P + E
    TABW = TILES + 4
    ROW = D + E
    RING = 4
    LO_BY_DVE = 5
    assert B % 2 == 0 and TILES % 2 == 0 and TILES <= 2 * P and E <= 32 and 2 * FREST == P

    rows = nc.dram_tensor("rows", [N + P, ROW], F32, kind="Internal").ap()

    with ExitStack() as ctx:
        def sb(name, shape, dt=F32):
            return ctx.enter_context(nc.sbuf_tensor(name, shape, dt))

        def ps(name, shape, dt=F32):
            return ctx.enter_context(nc.psum_tensor(name, shape, dt))

        def sem(name):
            return ctx.enter_context(nc.semaphore(name))

        front = Linear()
        front.chunks = DC; front.width = D; front.at = 0
        front.w_in = sb("w1_in", [P, DC, D])
        front.cmax = sb("f_cmax", [P, 2, D])
        front.grid = sb("f_grid", [P, 2, TT, D])
        front.qT = sb("f_qT", [P, 2, DC, T], BF16)
        front.wscale = sb("f_wscale", [P, D])
        front.s_row = sb("f_s_row", [P, D])
        front.prod = sb("f_prod", [P, TT, D])
        back = Linear()
        back.chunks = IC; back.width = I; back.at = 1
        back.w_in = sb("w2_in", [P, DC, I])
        back.cmax = sb("b_cmax", [P, 2, I])
        back.grid = sb("b_grid", [P, 2, TT, I])
        back.qT = sb("b_qT", [P, 2, IC, T], BF16)
        back.wscale = sb("b_wscale", [P, D])
        back.s_row = sb("b_s_row", [P, I])
        back.prod = sb("b_prod", [P, TT, D])
        for v in (front, back):
            v.am = sb(f"am{v.at}", [P, 2, v.chunks])
            v.ramw = sb(f"ramw{v.at}", [P, v.chunks])
            v.ratio = sb(f"ratio{v.at}", [P, v.chunks])
            v.root = sb(f"root{v.at}", [P, v.chunks])
            v.rroot = sb(f"rroot{v.at}", [P, v.chunks])
            v.sv = sb(f"sv{v.at}", [P, 2, v.chunks])
            v.rmax = sb(f"rmax{v.at}", [P, 2, TT])
            v.rscale = sb(f"rscale{v.at}", [P, 2, TT])
            v.rq = sb(f"rq{v.at}", [P, 2, TT])
            v.bn = sb(f"bn{v.at}", [P, TT, 6])
            v.mv = sb(f"mv{v.at}", [P, TT, 2])
            v.veps = sb(f"veps{v.at}", [P, TT])
            v.rstd = sb(f"rstd{v.at}", [P, TT])
            v.nmr = sb(f"nmr{v.at}", [P, TT])
        sg = sb("sg", [P, TT, I])
        x2n = sb("x2n", [P, TT, D])
        x2nT = sb("x2nT", [P, TT, DC, P])
        half = sb("half", [P, 8])
        neghalf = sb("neghalf", [P, 8])
        magic = sb("magic", [P, 1])
        nmagic = sb("nmagic", [P, 1])
        gates = sb("gates", [P, 2])
        tg = sb("tg", [P, 2])
        ident = sb("ident", [P, P])
        gwT = sb("gwT", [P, DC, E])
        zrow = sb("zrow", [P, ROW])
        L = sb("L", [P, TT, E])
        Lc = sb("Lc", [P, TT, E])
        eL = sb("eL", [P, TT, E])
        sumL = sb("sumL", [P, TT])
        rsumL = sb("rsumL", [P, TT])
        top = sb("top", [P, TT, TOP_K])
        topc = sb("topc", [P, TT, TOP_K])
        idx = sb("idx", [P, TT, TOP_K], U32)
        idxf = sb("idxf", [P, TT, TOP_K])
        tv = sb("tv", [P, TT, TOP_K])
        ssum = sb("ssum", [P, TT])
        rsum = sb("rsum", [P, TT])
        ren = sb("ren", [P, TT, TOP_K])
        cum = sb("cum", [P, TT, TOP_K])
        carry = sb("carry", [P, TT, TOP_K])
        active = sb("active", [P, NK, TOP_K])
        rw = sb("rw", [P, TT, TOP_K])
        keep = sb("keep", [P, TT, TOP_K])
        onehot = sb("onehot", [P, NK, TOP_K, E], BF16)
        prod = sb("prod", [P, TT, TOP_K, E])
        comb = sb("comb", [P, TT, E])
        member = sb("member", [P, NK, E], BF16)
        iota_e = sb("iota_e", [P, E])
        tri = sb("tri", [P, P], BF16)
        ones = sb("ones", [P, P], BF16)
        spare = back.prod[:].rearrange("p t d -> p (t d)")
        tot, pre_a, pre_b, slot_e = (spare[:, n * NK * E:(n + 1) * NK * E].rearrange("p (k e) -> p k e", e=E) for n in range(4))
        pre = [pre_a, pre_b]
        cnt_i = sb("cnt_i", [P, E], I32)
        tiles_f = sb("tiles_f", [P, E])
        tend = sb("tend", [P, E])
        tend_i = sb("tend_i", [P, E], I32)
        trips_i = sb("trips_i", [P, 1], I32)
        base_e = sb("base_e", [P, E])
        begin_i = sb("begin_i", [P, TABW], I32)
        one_e = sb("one_e", [P, E])
        pidx = sb("pidx", [P, 2])
        eid_c = sb("eid_c", [P, 2])
        cmp = sb("cmp", [P, E])
        eid_f = sb("eid_f", [P, 2 * P])
        eid_i = sb("eid_i", [P, 2 * P], I32)
        spare = back.grid[:].rearrange("p g t d -> p (g t d)")
        slot_f, slot_i, lo_i, hi_i = (spare[:, n * NK * TOP_K:(n + 1) * NK * TOP_K] for n in range(4))
        slot_f = slot_f.rearrange("p (k j) -> p k j", j=TOP_K)
        slot_i, lo_i, hi_i = slot_i.bitcast(I32), lo_i.bitcast(I32), hi_i.bitcast(I32)
        lo_h = sb("lo_h", [P, NK * TOP_K], FP16)
        hi_h = sb("hi_h", [P, NK * TOP_K], FP16)
        iota_lo = sb("iota_lo", [P, P], FP16)
        iota_hi = sb("iota_hi", [P, TILES], FP16)
        label = sb("label", [P, NK])
        spare = front.qT[:].rearrange("p g c t -> p (g c t)").bitcast(FP16)
        oh_lo, oh_label = (spare[:, n * 2 * TOP_K * P:(n + 1) * 2 * TOP_K * P].rearrange("p (r j n) -> p r j n", j=TOP_K, n=P)
                           for n in range(2))
        spare = front.grid[:].rearrange("p g t d -> p (g t d)").bitcast(FP16)
        oh_hi = spare[:, 0:2 * TOP_K * TILES].rearrange("p (r j n) -> p r j n", j=TOP_K, n=TILES)
        lo_f = sb("lo_f", [P, NK * TOP_K])
        lo_now = [sb(f"lo_now{r}", [P, TOP_K - LO_BY_DVE]) for r in range(2)]
        pad = sb("pad", [P, TILES])
        tok_f = sb("tok_f", [P, TABW])
        tok_i = sb("tok_i", [P, TABW], I32)
        wgu = sb("wgu", [P, RING, DC, GU])
        wd = sb("wd", [P, RING, 2, D])
        tok_now = [sb(f"tok_now{q}", [P, 4], I32) for q in range(2)]
        tok_out = [sb(f"tok_out{q}", [P, 4], I32) for q in range(2)]
        got = [sb(f"got{q}", [P, ROW]) for q in range(2)]
        wt = sb("wt", [P, TABW])
        pick = [sb(f"pick{q}", [P, E]) for q in range(2)]
        spare = front.grid[:].rearrange("p g t d -> p (g t d)")
        at = [0]

        def carve(n):
            at[0] += n
            return spare[:, at[0] - n:at[0]]

        gT = [carve(DC * P).rearrange("p (c t) -> p c t", c=DC) for q in range(2)]
        gs = [carve(F) for q in range(2)]
        hh = [carve(2 * P) for q in range(2)]
        yy = [carve(D) for q in range(2)]

        with ExitStack() as entries_only:
            x_in = entries_only.enter_context(nc.sbuf_tensor("x_in", [P, B, TT, D], F32))

        hT_high, hT_low = ([sb(f"hT_{part}{q}", [P, 2, P], F32R) for q in range(2)] for part in ("high", "low"))
        d_high = sb("d_high", [P, RING, 2, D], F32R)
        d_low = sb("d_low", [P, RING, D], F32R)

        pA = [ps(f"pA{i}", [P, 512]) for i in range(2)]
        pB = [ps(f"pB{i}", [P, 512]) for i in range(2)]
        pT = [ps(f"pT{i}", [P, 512]) for i in range(2)]
        pH = [ps(f"pH{i}", [P, 512]) for i in range(2)]

        front.bank = [pA[0], pA[1]]
        front.stage = [pT[0], pT[1]]
        front.out = [pB[0], pA[1]]
        back.bank = [pH[0], pH[0]]
        back.stage = [pB[1], pH[1]]
        back.out = [pH[1], pH[0]]

        consts_loaded = sem("consts_loaded")
        pool_consts = sem("pool_consts")
        act_consts = sem("act_consts")
        vec = sem("vec")
        x_loaded = sem("x_loaded")
        for v, side in ((front, "f"), (back, "b")):
            v.w_loaded = sem(f"{side}_w_loaded")
            v.var_ready = sem(f"{side}_var_ready")
            v.rstd_ready = sem(f"{side}_rstd_ready")
            v.nmr_ready = sem(f"{side}_nmr_ready")
            v.x_ready = sem(f"{side}_x_ready")
            v.cmax_ready = sem(f"{side}_cmax_ready")
            v.cmaxT_ready = sem(f"{side}_cmaxT_ready")
            v.ratio_ready = sem(f"{side}_ratio_ready")
            v.root_ready = sem(f"{side}_root_ready")
            v.s_ready = sem(f"{side}_s_ready")
            v.bcast_ready = sem(f"{side}_bcast_ready")
            v.s_row_ready = sem(f"{side}_s_row_ready")
            v.w_scaled = sem(f"{side}_w_scaled")
            v.scaled_ready = sem(f"{side}_scaled_ready")
            v.wscale_ready = sem(f"{side}_wscale_ready")
            v.wscale_copied = sem(f"{side}_wscale_copied")
            v.is_rounded = sem(f"{side}_is_rounded")
            v.staged = sem(f"{side}_staged")
            v.unstaged = sem(f"{side}_unstaged")
            v.product = sem(f"{side}_product")
            v.product_used = sem(f"{side}_product_used")
        silu_ready = sem("silu_ready")
        x2_ready = sem("x2_ready")
        x2n_ready = sem("x2n_ready")
        logits_ready = sem("logits_ready")
        logits_copied = sem("logits_copied")
        shifted = sem("shifted")
        exp_ready = sem("exp_ready")
        comb_ready = sem("comb_ready")
        x2_stored = sem("x2_stored")
        x2n_stored = sem("x2n_stored")
        comb_stored = sem("comb_stored")
        ranks_ready = sem("ranks_ready")
        eid_ready = sem("eid_ready")
        eidT_ready = sem("eidT_ready")
        plan_ready = sem("plan_ready")
        slot_e_ready = sem("slot_e_ready")
        products_ready = sem("products_ready")
        lo_ready = sem("lo_ready")
        lo_copied = sem("lo_copied")
        lo_hots = sem("lo_hots")
        pool_hots = sem("pool_hots")
        labelled = sem("labelled")
        hi_hots = sem("hi_hots")
        hot_used = sem("hot_used")
        tab_ready = sem("tab_ready")
        tok_ready = sem("tok_ready")
        w_landed = [sem(f"w_landed{r}") for r in range(RING)]
        weights_ready = sem("weights_ready")
        passed = sem("passed")
        out_idx_ready = sem("out_idx_ready")
        idx_ready = sem("idx_ready")
        gathered = [sem(f"gathered{q}") for q in range(2)]
        gT_filled = sem("gT_filled")
        gT_ready = sem("gT_ready")
        gu_ready = sem("gu_ready")
        gs_ready = sem("gs_ready")
        hh_ready = sem("hh_ready")
        wt_ready = sem("wt_ready")
        hT_filled = sem("hT_filled")
        hT_high_ready = sem("hT_high_ready")
        hT_low_ready = sem("hT_low_ready")
        dup_ready = sem("dup_ready")
        high_ready = sem("high_ready")
        low_ready = sem("low_ready")
        y_filled = sem("y_filled")
        y_ready = sem("y_ready")
        added = [sem(f"added{q}") for q in range(2)]
        additions = sem("additions")

        def choice_slots(b):
            return x_in[:, b].rearrange("p t d -> p (t d)")[:, 0:TT * TOP_K * E].rearrange("p (t j e) -> p t j e", t=TT, j=TOP_K)

        def x_rows(b, t):
            return x_in[:, bass.ds(b, 1), t, :].rearrange("p a d -> p (a d)")

        block = ctx.enter_context(nc.Block())

        @block.sync
        def _(sp):
            sp.dma_start(gwT[:], gate_w.rearrange("(c p) e -> p c e", p=P)).then_inc(consts_loaded, 16)
            sp.dma_start(gates[:, 0:1], g_x).then_inc(consts_loaded, 16)
            sp.dma_start(gates[:, 1:2], g_f).then_inc(consts_loaded, 16)

            def load_x(b):
                if b > 0:
                    sp.wait_ge(x_loaded, 16 * b)
                sp.dma_start(x_in[:, b], x[b].rearrange("(t p) d -> p t d", p=P)).then_inc(x_loaded, 16)

            def load_w(v, b):
                src = w1 if v is front else w2
                sp.dma_start(v.w_in[:], src[bass.ds(b, 1)].rearrange("a (t p) d -> p (a t) d", p=P)).then_inc(v.w_loaded, 16)

            def next_w(v, b):
                sp.wait_ge(v.w_scaled, DC * b + DC)
                load_w(v, b + 1)

            def store_x2(b):
                sp.wait_ge(x2_ready, TT * b + TT)
                sp.sem_inc(passed, 1)
                sp.dma_start(out[bass.ds(b * T, T), :].rearrange("(t p) d -> p t d", p=P),
                             back.prod[:]).then_inc(x2_stored, 16)

            def store_rows(b):
                sp.wait_ge(x2n_ready, TT * b + TT)
                sp.dma_start(rows[bass.ds(b * T, T), 0:D].rearrange("(t p) d -> p t d", p=P), x2n[:]).then_inc(x2n_stored, 16)
                sp.wait_ge(comb_ready, b + 1)
                sp.dma_start(rows[bass.ds(b * T, T), D:ROW].rearrange("(t p) d -> p t d", p=P), comb[:]).then_inc(comb_stored, 16)

            def load_expert(e, r):
                for c in range(DC):
                    sp.dma_start(wgu[:, r, c, :], gate_up_t[bass.ds(e, 1), c * P:(c + 1) * P, :].rearrange("a p n -> p (a n)")
                                 ).then_inc(w_landed[r], 16)
                sp.dma_start(wd[:, r, 0, :], down_t[bass.ds(e, 1), 0:P, :].rearrange("a p n -> p (a n)")).then_inc(w_landed[r], 16)
                for side in range(2):
                    sp.dma_start(wd[side * FREST:(side + 1) * FREST, r, 1, :],
                                 down_t[bass.ds(e, 1), P:F, :].rearrange("a p n -> p (a n)")).then_inc(w_landed[r], 16)

            load_x(0)
            load_w(front, 0)
            load_x(1)
            load_w(back, 0)
            next_w(front, 0)
            for b in range(2, B):
                load_x(b)
            for r in range(RING):
                load_expert(r, r)
            with sp.Fori(0, B - 2) as b:
                next_w(back, b)
                next_w(front, b + 1)
                store_x2(b)
                store_rows(b)
            next_w(back, B - 2)
            for b in (B - 2, B - 1):
                store_x2(b)
                store_rows(b)

            def announce(r, times):
                sp.wait_ge(w_landed[r], 16 * (DC + 3) * times)
                sp.sem_inc(weights_ready, 1)

            for r in range(RING - 1):
                announce(r, 1)
            sp.wait_ge(plan_ready, 1)
            with sp.Fori(0, E // RING - 1) as it:
                for r in range(RING):
                    e = it * RING + r
                    last = nc.sync.value_load(tend_i[0:1, bass.ds(e, 1)], min_val=1, max_val=TILES)
                    sp.wait_ge(y_filled, last + 2)
                    load_expert(e + RING, r)
                    announce((r - 1) % RING, it + (1 if r == 0 else 2))
            announce(RING - 1, E // RING)
            sp.wait_ge(x2_stored, 16 + 16 * B)
            sp.wait_ge(x2n_stored, 16 + 16 * B)
            sp.wait_ge(comb_stored, 16 + 16 * B)

        @block.gpsimd
        def _(pool):
            pool.memset(zrow[:], 0.0).then_inc(pool_consts, 1)
            pool.memset(half[:], 0.5).then_inc(pool_consts, 1)
            pool.memset(neghalf[:], -0.5).then_inc(pool_consts, 1)
            pool.memset(magic[:], MAGIC).then_inc(pool_consts, 1)
            pool.memset(nmagic[:], -MAGIC).then_inc(pool_consts, 1)
            pool.memset(ones[:], 1.0).then_inc(pool_consts, 1)
            pool.memset(one_e[:], 1.0).then_inc(pool_consts, 1)
            pool.memset(ident[:], 0.0).then_inc(pool_consts, 1)
            pool.memset(carry[:], 1.0).then_inc(pool_consts, 1)
            pool.iota(iota_e[:], [[1, E]], base=0, channel_multiplier=0,
                      allow_small_or_imprecise_dtypes=True).then_inc(pool_consts, 1)
            pool.iota(iota_lo[:], [[1, P]], base=0, channel_multiplier=0,
                      allow_small_or_imprecise_dtypes=True).then_inc(pool_consts, 1)
            pool.iota(iota_hi[:], [[1, TILES]], base=0, channel_multiplier=0,
                      allow_small_or_imprecise_dtypes=True).then_inc(pool_consts, 1)
            pool.iota(pidx[:], [[P, 2]], base=0, channel_multiplier=1,
                      allow_small_or_imprecise_dtypes=True).then_inc(pool_consts, 1)
            pool.iota(label[:], [[-P, NK]], base=N, channel_multiplier=-1,
                      allow_small_or_imprecise_dtypes=True).then_inc(pool_consts, 1)
            pool.wait_ge(pool_consts, 14)
            pool.affine_select(out=ident[:], in_=ident[:], compare_op=ALU.not_equal, fill=1.0,
                               base=0, pattern=[[-1, P]], channel_multiplier=1).then_inc(pool_consts, 1)
            pool.affine_select(out=tri[:], in_=ones[:], compare_op=ALU.is_gt, fill=0.0,
                               base=0, pattern=[[1, P]], channel_multiplier=-1).then_inc(pool_consts, 1)
            pool.affine_select(out=carry[:], in_=carry[:], compare_op=ALU.not_equal, fill=0.0,
                               base=0, pattern=[[0, TT], [1, TOP_K]], channel_multiplier=0).then_inc(pool_consts, 1)

            pool.dma_start(rows[N:N + P, :], zrow[:]).then_inc(added[0], 16)
            pool.dma_start(out[N:N + P, :], zrow[:, 0:D]).then_inc(added[1], 16)

            def inverse_std(v, b):
                pool.wait_ge(v.var_ready, b + 1)
                pool.tensor_tensor(v.rstd[:], v.veps[:], neghalf[:, 0:TT], ALU.pow).then_inc(v.rstd_ready, 1)

            def square_root(v, b):
                pool.wait_ge(v.ratio_ready, b + 1)
                pool.tensor_tensor(v.root[:], v.ratio[:], half[:, 0:v.chunks], ALU.pow).then_inc(v.root_ready, 1)

            def scale_weights(v, b):
                pool.wait_ge(v.s_row_ready, b + 1)
                for t in range(DC):
                    pool.tensor_tensor(v.grid[:, 1, t, :], v.w_in[:, t, :], v.s_row[:], ALU.mult).then_inc(v.w_scaled, 1)

            def gate_times_up(b):
                for t in range(TT):
                    pool.wait_ge(silu_ready, TT * b + t + 1)
                    pool.tensor_tensor(back.grid[:, 0, t, :], sg[:, t, :], front.prod[:, t, I:2 * I], ALU.mult).then_inc(back.x_ready, 1)

            def residual(b):
                for t in range(TT):
                    pool.wait_ge(back.product_used, TT * b + t + 3)
                    pool.tensor_tensor(back.prod[:, t, :], back.prod[:, t, :], x_rows(b, t), ALU.add).then_inc(x2_ready, 1)

            def normalise_second(b):
                pool.wait_ge(back.nmr_ready, b + 1)
                pool.wait_ge(x2n_stored, 16 * b + 16)
                pool.sem_inc(passed, 1)
                for t in range(TT):
                    pool.tensor_scalar(x2n[:, t, :], back.prod[:, t, :], back.rstd[:, t:t + 1], back.nmr[:, t:t + 1],
                                       ALU.mult, ALU.add).then_inc(x2n_ready, 1)

            def entries(b, last):
                residual(b)
                if not last:
                    inverse_std(front, b + 2)
                inverse_std(back, b)
                normalise_second(b)
                gate_times_up(b + 1)
                if not last:
                    square_root(front, b + 2)
                square_root(back, b + 1)
                scale_weights(back, b + 1)
                if not last:
                    scale_weights(front, b + 2)

            inverse_std(front, 0)
            square_root(front, 0)
            scale_weights(front, 0)
            inverse_std(front, 1)
            gate_times_up(0)
            square_root(front, 1)
            square_root(back, 0)
            scale_weights(back, 0)
            scale_weights(front, 1)
            with pool.Fori(0, B - 2) as b:
                entries(b, False)
            entries(B - 2, True)
            residual(B - 1)
            inverse_std(back, B - 1)

            pool.wait_ge(slot_e_ready, 1)
            for b in range(1, B, 2):
                pool.tensor_tensor(choice_slots(b), onehot[:, b * TT:(b + 1) * TT, :, :],
                                   slot_e[:, b * TT:(b + 1) * TT, :].unsqueeze(2).to_broadcast([P, TT, TOP_K, E]),
                                   ALU.mult).then_inc(products_ready, 1)

            pool.wait_ge(lo_ready, 1)
            LO_BY_POOL = TOP_K - LO_BY_DVE
            with pool.Fori(0, NK // 2) as it:
                for r in range(2):
                    k = 2 * it + r
                    pool.wait_ge(labelled, k + 1)
                    pool.sem_inc(passed, 1)
                    pool.tensor_copy(lo_now[r][:], lo_f[:, bass.ds(TOP_K * k + LO_BY_DVE, LO_BY_POOL)]).then_inc(lo_copied, 1)
                    pool.wait_ge(lo_copied, k + 1)
                    pool.sem_inc(passed, 1)
                    for j in range(LO_BY_POOL):
                        pool.tensor_scalar(oh_lo[:, r, LO_BY_DVE + j, :], iota_lo[:], lo_now[r][:, j:j + 1], None,
                                           ALU.is_equal).then_inc(pool_hots, 1)

            pool.wait_ge(tok_ready, 1)
            pool.wait_ge(x2_stored, 16 + 16 * B)
            pool.wait_ge(x2n_stored, 16 + 16 * B)
            pool.wait_ge(comb_stored, 16 + 16 * B)
            pool.wait_ge(added[0], 16)
            pool.wait_ge(added[1], 16)

            def gather(i, q):
                pool.tensor_copy(tok_now[q][:, 0:1], tok_i[:, bass.ds(i, 1)]).then_inc(idx_ready, 1)
                pool.wait_ge(idx_ready, i + 1)
                pool.sem_inc(passed, 1)
                pool.indirect_dma_start(out=got[q][:], out_offset=None, in_=rows,
                                        in_offset=bass.IndirectOffsetOnAxis(ap=tok_now[q][:, 0:1], axis=0)
                                        ).then_inc(gathered[q], 16)

            def add_rows(i, q, before):
                pool.wait_ge(added[1 - q], before)
                pool.sem_inc(additions, 1)
                pool.tensor_copy(tok_out[q][:, 0:1], tok_i[:, bass.ds(i, 1)]).then_inc(out_idx_ready, 1)
                pool.wait_ge(out_idx_ready, i + 1)
                pool.wait_ge(y_ready, i + 3)
                pool.sem_inc(passed, 1)
                pool.indirect_dma_start(out=out, out_offset=bass.IndirectOffsetOnAxis(ap=tok_out[q][:, 0:1], axis=0),
                                        in_=yy[q], in_offset=None, compute_op=ALU.add
                                        ).then_inc(added[q], 16)

            pool.sem_inc(additions, 1)
            gather(0, 0)
            gather(1, 1)
            for i in range(2):
                pool.wait_ge(gT_filled, i + 1)
                pool.wait_ge(wt_ready, i + 1)
                gather(i + 2, i)
            trips = nc.gpsimd.value_load(trips_i[0:1, 0:1], min_val=1, max_val=TILES // 2)
            with pool.Fori(0, trips) as it:
                for q in range(2):
                    i = 2 * it + q
                    pool.wait_ge(gT_filled, i + 3)
                    pool.wait_ge(wt_ready, i + 3)
                    gather(i + 4, q)
                    add_rows(i, q, 16 * it + 16 * (q + 1))
            pool.wait_ge(added[0], 16 * trips + 16)
            pool.wait_ge(added[1], 16 * trips + 16)
            pool.wait_ge(gathered[0], 16 * trips + 32)
            pool.wait_ge(gathered[1], 16 * trips + 32)

        @block.scalar
        def _(act_e):
            act_e.sem_inc(front.unstaged, 2)
            act_e.sem_inc(back.unstaged, 2)
            act_e.sem_inc(y_ready, 2)
            act_e.wait_ge(consts_loaded, 48)
            nc.scalar.activation(tg[:], gates[:], ACT.Tanh).then_inc(act_consts, 1)
            act_e.wait_ge(act_consts, 1)
            act_e.wait_ge(pool_consts, 5)

            def normalise(v, b):
                act_e.wait_ge(v.nmr_ready, b + 1)
                if v is back:
                    act_e.wait_ge(x2n_stored, 16 * b + 16)
                for t in range(TT):
                    if v is front:
                        nc.scalar.activation(front.grid[:, 0, t, :], x_rows(b, t),
                                             ACT.Identity, bias=v.nmr[:, t:t + 1], scale=v.rstd[:, t:t + 1]).then_inc(front.x_ready, 1)
                    else:
                        nc.scalar.activation(x2n[:, t, :], back.prod[:, t, :], ACT.Identity, bias=v.nmr[:, t:t + 1],
                                             scale=v.rstd[:, t:t + 1]).then_inc(x2n_ready, 1)

            def copy_s(v, b):
                act_e.wait_ge(v.bcast_ready, b + 1)
                lo = 0 if v is front else I
                nc.scalar.activation(v.s_row[:], v.bank[1][:, lo:lo + v.width], ACT.Copy).then_inc(v.s_row_ready, 1)

            def round_rows(v, b):
                act_e.wait_ge(v.scaled_ready, b + 1)
                for g in range(2):
                    for t in range(TT):
                        nc.scalar.activation(v.grid[:, g, t, :], v.grid[:, g, t, :], ACT.Identity,
                                             bias=magic[:, 0:1], scale=v.rq[:, g, t:t + 1]).then_inc(v.is_rounded, 1)

            def copy_wscale(v, b):
                act_e.wait_ge(v.wscale_ready, b + 1)
                if v is front:
                    nc.scalar.activation(v.wscale[:], v.bank[0][:], ACT.Copy).then_inc(v.wscale_copied, 1)
                else:
                    nc.scalar.activation(v.wscale[:], v.stage[1][:], ACT.Copy, scale=tg[:, 0:1]).then_inc(v.wscale_copied, 1)

            def unstage(v, b):
                for g in range(2):
                    for c in range(v.chunks):
                        k = g * v.chunks + c
                        act_e.wait_ge(v.staged, 8 * b + k + 1)
                        nc.scalar.activation(v.qT[:, g, c, :], v.stage[k % 2][:], ACT.Identity,
                                             bias=nmagic[:, 0:1], scale=1.0).then_inc(v.unstaged, 1)

            def tokens_across(b):
                for t in range(TT):
                    k = 2 * IC + t
                    act_e.wait_ge(back.staged, 8 * b + k + 1)
                    nc.scalar.activation(x2nT[:, t], back.stage[k % 2][:].rearrange("p (c t) -> p c t", c=DC), ACT.Copy).then_inc(back.unstaged, 1)
                act_e.wait_ge(logits_ready, b + 1)
                nc.scalar.activation(L[:], front.out[0][:, 0:TT * E].rearrange("p (t e) -> p t e", e=E), ACT.Copy).then_inc(logits_copied, 1)

            def silu_gate_half(b):
                for t in range(TT):
                    act_e.wait_ge(front.product_used, TT * b + t + 3)
                    nc.scalar.activation(sg[:, t, :], front.prod[:, t, 0:I], ACT.Silu).then_inc(silu_ready, 1)

            def exponentials(b):
                act_e.wait_ge(shifted, b + 1)
                nc.scalar.activation(eL[:], Lc[:], ACT.Exp).then_inc(exp_ready, 1)
                nc.scalar.activation(tv[:], topc[:], ACT.Exp).then_inc(exp_ready, 1)

            normalise(front, 0)
            copy_s(front, 0)
            round_rows(front, 0)
            copy_wscale(front, 0)
            unstage(front, 0)
            normalise(front, 1)
            silu_gate_half(0)
            copy_s(back, 0)
            copy_s(front, 1)

            def entries(b, last):
                round_rows(back, b)
                copy_wscale(back, b)
                unstage(back, b)
                round_rows(front, b + 1)
                copy_wscale(front, b + 1)
                unstage(front, b + 1)
                if not last:
                    normalise(front, b + 2)
                silu_gate_half(b + 1)
                tokens_across(b)
                exponentials(b)
                copy_s(back, b + 1)
                if not last:
                    copy_s(front, b + 2)

            with act_e.Fori(0, B - 2) as b:
                entries(b, False)
            entries(B - 2, True)
            round_rows(back, B - 1)
            copy_wscale(back, B - 1)
            unstage(back, B - 1)
            normalise(back, B - 1)
            tokens_across(B - 1)
            exponentials(B - 1)

            with act_e.Fori(0, NK // 2) as it:
                for r in range(2):
                    k = 2 * it + r
                    act_e.wait_ge(lo_hots, k + 1)
                    act_e.wait_ge(pool_hots, (TOP_K - LO_BY_DVE) * (k + 1))
                    act_e.wait_ge(hot_used, k + 1)
                    act_e.sem_inc(passed, 1)
                    nc.scalar.activation(oh_label[:, r], oh_lo[:, r], ACT.Copy, scale=label[:, bass.ds(k, 1)]).then_inc(labelled, 1)

            act_e.wait_ge(tok_ready, 1)

            def rows_across(i, q):
                act_e.wait_ge(gT_filled, i + 1)
                nc.scalar.activation(gT[q], pT[q][:].rearrange("p (c t) -> p c t", c=DC), ACT.Copy).then_inc(gT_ready, 1)

            def begins(i):
                return nc.scalar.value_load(begin_i[0:1, bass.ds(i, 1)], min_val=0, max_val=E)

            def high_parts(e):
                act_e.wait_ge(weights_ready, e + 1)
                act_e.sem_inc(passed, 1)
                nc.scalar.activation(d_high[:, bass.ds(e % RING, 1)], wd[:, bass.ds(e % RING, 1)], ACT.Copy).then_inc(high_ready, 1)

            def inner_across(i, q):
                act_e.wait_ge(hT_filled, i + 1)
                act_e.wait_ge(y_filled, i + 1)
                nc.scalar.activation(hT_high[q][:], pA[q][:, 0:2 * P].rearrange("p (c t) -> p c t", c=2), ACT.Copy).then_inc(hT_high_ready, 1)

            def silu_gate(i, q):
                act_e.wait_ge(gu_ready, i + 1)
                nc.scalar.activation(gs[q], pH[q][:, 0:F], ACT.Silu).then_inc(gs_ready, 1)

            def weigh_rows(i, q):
                act_e.wait_ge(y_filled, i + 3)
                act_e.wait_ge(additions, i + 1)
                nc.scalar.activation(yy[q], pB[q][:], ACT.Copy, scale=wt[:, bass.ds(i, 1)]).then_inc(y_ready, 1)

            trips = nc.scalar.value_load(trips_i[0:1, 0:1], min_val=1, max_val=TILES // 2)
            high_parts(0)
            begin = begins(1)
            rows_across(0, 0)
            rows_across(1, 1)
            with act_e.If(begin != 0):
                high_parts(begin - 1)
            silu_gate(0, 0)
            with act_e.Fori(0, trips) as it:
                for i, q in ((2 * it + 1, 1), (2 * it + 2, 0)):
                    inner_across(i - 1, 1 - q)
                    rows_across(i + 1, 1 - q)
                    begin = begins(i + 1)
                    with act_e.If(begin != 0):
                        high_parts(begin - 1)
                    silu_gate(i, q)
                    act_e.wait_ge(wt_ready, i)
                    weigh_rows(i - 1, 1 - q)

        @block.tensor
        def _(pe):
            pe.wait_ge(pool_consts, 17)
            pe.wait_ge(consts_loaded, 48)
            pe.sem_inc(y_filled, 2)

            def column_maxima(v, b):
                pe.wait_ge(v.cmax_ready, 2 * b + 2)
                for g in range(2):
                    for c in range(v.chunks):
                        at = (c if v is front else g * v.chunks + c) * P
                        mm = nc.tensor.transpose(v.bank[g][:, at:at + P], v.cmax[:, g, c * P:(c + 1) * P], ident[:])
                mm.then_inc(v.cmaxT_ready, 1)

            def spread(dst, col):
                return nc.tensor.matmul(dst, col.to_broadcast([P, P]), ident[:], start=True, stop=True)

            def column_scales(v, b):
                pe.wait_ge(v.s_ready, b + 1)
                for g in range(2):
                    for c in range(v.chunks):
                        at = (c if v is front else g * v.chunks + c) * P
                        mm = spread(v.bank[g][:, at:at + P], v.sv[:, g, c:c + 1])
                mm.then_inc(v.bcast_ready, 1)

            def weight_scales(v, b):
                pe.wait_ge(v.scaled_ready, b + 1)
                dst = v.bank[0] if v is front else v.stage[1]
                for t in range(DC):
                    mm = spread(dst[:, t * P:(t + 1) * P], v.rscale[:, 1, t:t + 1])
                mm.then_inc(v.wscale_ready, 1)

            def stage_columns(v, b):
                for g in range(2):
                    for c in range(v.chunks):
                        k = g * v.chunks + c
                        pe.wait_ge(v.unstaged, 8 * b + k + 1)
                        if v is back and k == 1:
                            pe.wait_ge(back.wscale_copied, b + 1)
                        for t in range(TT):
                            if c == 0:
                                pe.wait_ge(v.is_rounded, 8 * b + 4 * g + t + 1)
                            mm = nc.tensor.transpose(v.stage[k % 2][:, t * P:(t + 1) * P],
                                                     v.grid[:, g, t, c * P:(c + 1) * P], ident[:])
                        mm.then_inc(v.staged, 1)

            def products(v, b):
                pe.wait_ge(v.unstaged, 8 * b + 2 * v.chunks + 2)
                if v is front and not (isinstance(b, int) and b == 0):
                    pe.wait_ge(logits_copied, b - 1)
                for t in range(TT):
                    pe.wait_ge(v.product_used, TT * b + t + 1)
                    for c in range(v.chunks):
                        mm = nc.tensor.matmul(v.out[t % 2][:], v.qT[:, 0, c, t * P:(t + 1) * P], v.qT[:, 1, c, :],
                                              start=(c == 0), stop=(c == v.chunks - 1))
                    mm.then_inc(v.product, 1)

            def logits(b):
                def rows_up(t):
                    k = 2 * IC + t
                    pe.wait_ge(x2n_ready, TT * b + t + 1)
                    pe.wait_ge(back.unstaged, 8 * b + k + 1)
                    for c in range(DC):
                        mm = nc.tensor.transpose(back.stage[k % 2][:, c * P:(c + 1) * P], x2n[:, t, c * P:(c + 1) * P], ident[:])
                    mm.then_inc(back.staged, 1)

                rows_up(0)
                for t in range(TT):
                    if t + 1 < TT:
                        rows_up(t + 1)
                    pe.wait_ge(back.unstaged, 8 * b + 2 * IC + t + 3)
                    for c in range(DC):
                        mm = nc.tensor.matmul(front.out[0][:, t * E:(t + 1) * E], x2nT[:, t, c, :], gwT[:, c, :],
                                              start=(c == 0), stop=(c == DC - 1))
                mm.then_inc(logits_ready, 1)

            column_maxima(front, 0)
            column_scales(front, 0)
            weight_scales(front, 0)
            stage_columns(front, 0)
            products(front, 0)
            column_maxima(front, 1)
            column_maxima(back, 0)
            column_scales(back, 0)
            column_scales(front, 1)

            def entries(b, last):
                weight_scales(back, b)
                stage_columns(back, b)
                products(back, b)
                weight_scales(front, b + 1)
                stage_columns(front, b + 1)
                products(front, b + 1)
                logits(b)
                if not last:
                    column_maxima(front, b + 2)
                column_maxima(back, b + 1)
                column_scales(back, b + 1)
                if not last:
                    column_scales(front, b + 2)

            with pe.Fori(0, B - 2) as b:
                entries(b, False)
            entries(B - 2, True)
            weight_scales(back, B - 1)
            stage_columns(back, B - 1)
            products(back, B - 1)
            logits(B - 1)

            pe.wait_ge(comb_ready, B)
            mflat = member[:].rearrange("p k e -> p (k e)")
            nc.tensor.matmul(pA[0][:], tri[:], mflat, start=True, stop=True)
            nc.tensor.matmul(pA[1][:], ones[:], mflat, start=True, stop=True).then_inc(ranks_ready, 1)
            pe.wait_ge(eid_ready, 1)
            for g in range(2):
                mm = spread(pB[0][:, g * P:(g + 1) * P], eid_c[:, g:g + 1])
            mm.then_inc(eidT_ready, 1)
            zero_lo, zero_hi = zrow[:, 0:P // 2].bitcast(FP16), zrow[:, 0:TILES // 2].bitcast(FP16)
            nc.tensor.matmul(pB[1][:, 0:TILES], zero_lo, zero_hi, start=True, stop=False, skip_group_check=True)
            with pe.Fori(0, NK // 2) as it:
                for r in range(2):
                    k = 2 * it + r
                    pe.wait_ge(labelled, k + 3)
                    pe.wait_ge(hi_hots, k + 1)
                    for j in range(TOP_K):
                        mm = nc.tensor.matmul(pB[1][:, 0:TILES], oh_label[:, r, j, :], oh_hi[:, r, j, :],
                                              start=False, stop=False, skip_group_check=True)
                    mm.then_inc(hot_used, 1)
            nc.tensor.matmul(pB[1][:, 0:TILES], zero_lo, zero_hi, start=False, stop=True,
                             skip_group_check=True).then_inc(tab_ready, 1)

            pe.wait_ge(tok_ready, 1)

            def rows_across(i, q):
                if q == 0:
                    pe.wait_ge(gathered[0], 8 * i + 16)
                else:
                    pe.wait_ge(gathered[1], 8 * i + 8)
                for c in range(DC):
                    mm = nc.tensor.transpose(pT[q][:, c * P:(c + 1) * P], got[q][:, c * P:(c + 1) * P], ident[:])
                mm.then_inc(gT_filled, 1)

            def expert_slot(i):
                e = nc.tensor.value_load(eid_i[0:1, bass.ds(i, 1)], min_val=0, max_val=E - 1)
                return e, nc.tensor.snap(e % RING, min_val=0, max_val=RING - 1)

            def gate_up(i, q, e, slot):
                pe.wait_ge(weights_ready, e + 1)
                pe.wait_ge(gT_ready, i + 1)
                for c in range(DC):
                    mm = nc.tensor.matmul(pH[q][:, 0:GU], gT[q][:, c, :], wgu[:, bass.ds(slot, 1), c, :],
                                          start=(c == 0), stop=(c == DC - 1))
                mm.then_inc(gu_ready, 1)

            def inner_across(i, q):
                pe.wait_ge(hh_ready, i + 1)
                nc.tensor.transpose(pA[q][:, 0:P], hh[q][:, 0:P], ident[:])
                pe.wait_ge(dup_ready, i + 1)
                nc.tensor.transpose(pA[q][:, P:2 * P], hh[q][:, P:2 * P], ident[:]).then_inc(hT_filled, 1)

            def down(i, q, e, slot):
                pe.wait_ge(low_ready, 2 * e + 2)
                pe.wait_ge(hT_high_ready, i + 1)
                pe.wait_ge(y_ready, i + 1)
                dst = pB[q][:]
                nc.tensor.matmul(dst, hT_high[q][:, 0, :], d_high[:, bass.ds(slot, 1), 0, :], start=True, stop=False)
                nc.tensor.matmul(dst, hT_high[q][:, 0, :], d_low[:, bass.ds(slot, 1), :], start=False, stop=False)
                nc.tensor.matmul(dst, hT_high[q][:, 1, :], d_high[:, bass.ds(slot, 1), 1, :], start=False, stop=False)
                pe.wait_ge(hT_low_ready, i + 1)
                nc.tensor.matmul(dst, hT_low[q][:, 0, :], d_high[:, bass.ds(slot, 1), 0, :], start=False, stop=False)
                nc.tensor.matmul(dst, hT_low[q][0:FREST, 1, :], d_high[0:FREST, bass.ds(slot, 1), 1, :],
                                 start=False, stop=True).then_inc(y_filled, 1)

            trips = nc.tensor.value_load(trips_i[0:1, 0:1], min_val=1, max_val=TILES // 2)
            rows_across(0, 0)
            rows_across(1, 1)
            gate_up(0, 0, *expert_slot(0))
            with pe.Fori(0, trips) as it:
                i = 2 * it + 1
                first, second = expert_slot(i - 1), expert_slot(i)
                pe.wait_ge(gT_ready, i)
                rows_across(i + 1, 0)
                inner_across(i - 1, 0)
                gate_up(i, 1, *second)
                third = expert_slot(i + 1)
                down(i - 1, 0, *first)
                pe.wait_ge(gT_ready, i + 1)
                rows_across(i + 2, 1)
                inner_across(i, 1)
                gate_up(i + 1, 0, *third)
                down(i, 1, *second)

        @block.vector
        def _(dve):
            count = [0, 0]

            def step(ins):
                count[0] += 1
                return ins.then_inc(vec, 1)

            def settle():
                dve.wait_ge(vec, count[1] + count[0])

            dve.sem_inc(front.product_used, 2)
            dve.sem_inc(back.product_used, 2)
            dve.sem_inc(hot_used, 2)
            dve.sem_inc(labelled, 2)
            dve.sem_inc(x2_stored, 16)
            dve.sem_inc(x2n_stored, 16)
            dve.sem_inc(comb_stored, 16)
            dve.wait_ge(pool_consts, 17)

            def statistics(v, b):
                if v is front:
                    dve.wait_ge(x_loaded, 16 * b + 16)
                for t in range(TT):
                    if v is back:
                        dve.wait_ge(x2_ready, TT * b + t + 1)
                    step(nc.vector.bn_stats(v.bn[:, t, :], back.prod[:, t, :] if v is back else x_rows(b, t)))
                settle()
                dve.sem_inc(passed, 1)
                for t in range(TT):
                    step(nc.vector.bn_aggr(v.mv[:, t, :], v.bn[:, t, :]))
                settle()
                nc.vector.tensor_scalar(v.veps[:], v.mv[:, :, 1], EPS_LN, None, ALU.add).then_inc(v.var_ready, 1)

            def mean_over_std(v, b):
                dve.wait_ge(v.rstd_ready, b + 1)
                nc.vector.scalar_tensor_tensor(out=v.nmr[:], in0=v.mv[:, :, 0], scalar=-1.0, in1=v.rstd[:],
                                               op0=ALU.mult, op1=ALU.mult).then_inc(v.nmr_ready, 1)

            def weight_maxima(v, b):
                dve.wait_ge(v.w_loaded, 16 * b + 16)
                nc.vector.tensor_reduce(v.cmax[:, 1, :], v.w_in[:].rearrange("p t d -> p d t"), AX.X, ALU.max,
                                        apply_absolute_value=True).then_inc(v.cmax_ready, 1)

            def activation_maxima(v, b):
                dve.wait_ge(v.x_ready, TT * b + TT)
                nc.vector.tensor_reduce(v.cmax[:, 0, :], v.grid[:, 0].rearrange("p t d -> p d t"), AX.X, ALU.max,
                                        apply_absolute_value=True).then_inc(v.cmax_ready, 1)

            def column_ratio(v, b):
                dve.wait_ge(v.cmaxT_ready, b + 1)
                if v is front:
                    for g in range(2):
                        step(nc.vector.tensor_reduce(v.am[:, g, :], v.bank[g][:].rearrange("p (c t) -> p c t", t=P), AX.X, ALU.max))
                else:
                    step(nc.vector.tensor_reduce(v.am[:].rearrange("p g c -> p (g c)"), v.bank[0][:].rearrange("p (c t) -> p c t", t=P),
                                                 AX.X, ALU.max))
                settle()
                step(nc.vector.tensor_scalar(v.am[:], v.am[:], EPS_Q, None, ALU.max))
                settle()
                step(nc.vector.reciprocal(v.ramw[:], v.am[:, 1, :]))
                settle()
                nc.vector.tensor_tensor(v.ratio[:], v.am[:, 0, :], v.ramw[:], ALU.mult).then_inc(v.ratio_ready, 1)

            def column_scale(v, b):
                dve.wait_ge(v.root_ready, b + 1)
                step(nc.vector.reciprocal(v.rroot[:], v.root[:]))
                settle()
                step(nc.vector.tensor_tensor(v.rroot[:], v.ratio[:], v.rroot[:], ALU.mult))
                settle()
                step(nc.vector.tensor_tensor(v.rroot[:], v.root[:], v.rroot[:], ALU.add))
                settle()
                step(nc.vector.tensor_scalar(v.sv[:, 1, :], v.rroot[:], 0.5, EPS_Q, ALU.mult, ALU.max))
                settle()
                nc.vector.reciprocal(v.sv[:, 0, :], v.sv[:, 1, :]).then_inc(v.s_ready, 1)

            def scale_x(v, b):
                dve.wait_ge(v.bcast_ready, b + 1)
                if v is back:
                    dve.wait_ge(back.s_row_ready, b + 1)
                step(nc.vector.tensor_tensor(v.grid[:, 0], v.grid[:, 0],
                                             v.bank[0][:, 0:v.width].unsqueeze(1).to_broadcast([P, TT, v.width]), ALU.mult))

            def row_scales(v, b):
                settle()
                step(nc.vector.tensor_reduce(v.rmax[:, 0, :], v.grid[:, 0], AX.X, ALU.max, apply_absolute_value=True))
                dve.wait_ge(v.w_scaled, DC * b + DC)
                step(nc.vector.tensor_reduce(v.rmax[:, 1, :], v.grid[:, 1], AX.X, ALU.max, apply_absolute_value=True))
                settle()
                step(nc.vector.tensor_scalar(v.rscale[:], v.rmax[:], EPS_Q, 1.0 / QMAX, ALU.max, ALU.mult))
                settle()
                nc.vector.reciprocal(v.rq[:], v.rscale[:]).then_inc(v.scaled_ready, 1)

            def dequantise(v, b):
                dve.wait_ge(v.wscale_copied, b + 1)
                if v is back:
                    dve.wait_ge(x2_stored, 16 * b + 16)
                    dve.wait_ge(x2n_stored, 16 * b + 16)
                for t in range(TT):
                    dve.wait_ge(v.product, TT * b + t + 1)
                    nc.vector.scalar_tensor_tensor(out=v.prod[:, t, :], in0=v.out[t % 2][:], scalar=v.rscale[:, 0, t:t + 1],
                                                   in1=v.wscale[:], op0=ALU.mult, op1=ALU.mult).then_inc(v.product_used, 1)

            def choose(b):
                k0 = TT * b
                dve.wait_ge(logits_copied, b + 1)
                dve.sem_inc(passed, 1)
                for t in range(TT):
                    step(nc.vector.max(top[:, t, :], L[:, t, :]))
                settle()
                dve.sem_inc(passed, 1)
                for t in range(TT):
                    step(nc.vector.max_index(idx[:, t, :], top[:, t, :], L[:, t, :]))
                first = top[:, :, 0:1]
                step(nc.vector.tensor_tensor(Lc[:], L[:], first.to_broadcast([P, TT, E]), ALU.subtract))
                nc.vector.tensor_tensor(topc[:], top[:], first.to_broadcast([P, TT, TOP_K]), ALU.subtract).then_inc(shifted, 1)
                settle()
                step(nc.vector.tensor_copy(idxf[:], idx[:]))
                settle()
                step(nc.vector.tensor_tensor(
                    onehot[:, bass.ds(k0, TT), :, :],
                    iota_e[:].unsqueeze(1).unsqueeze(1).to_broadcast([P, TT, TOP_K, E]),
                    idxf[:].unsqueeze(3).to_broadcast([P, TT, TOP_K, E]), ALU.is_equal))

            def combine(b):
                k0 = TT * b
                dve.wait_ge(exp_ready, 2 * b + 2)
                step(nc.vector.tensor_reduce(sumL[:], eL[:], AX.X, ALU.add))
                settle()
                step(nc.vector.reciprocal(rsumL[:], sumL[:]))
                settle()
                step(nc.vector.tensor_tensor(tv[:], tv[:], rsumL[:].unsqueeze(2).to_broadcast([P, TT, TOP_K]), ALU.mult))
                settle()

                def normalised(dst, src):
                    step(nc.vector.tensor_reduce(ssum[:], src, AX.X, ALU.add))
                    settle()
                    step(nc.vector.tensor_scalar(ssum[:], ssum[:], SUM_FLOOR, None, ALU.max))
                    settle()
                    step(nc.vector.reciprocal(rsum[:], ssum[:]))
                    settle()
                    step(nc.vector.tensor_tensor(dst, src, rsum[:].unsqueeze(2).to_broadcast([P, TT, TOP_K]), ALU.mult))
                    settle()

                normalised(ren[:], tv[:])
                step(nc.vector.tensor_tensor_scan(cum[:].rearrange("p t j -> p (t j)"), carry[:].rearrange("p t j -> p (t j)"),
                                                  ren[:].rearrange("p t j -> p (t j)"), 0.0, ALU.mult, ALU.add))
                settle()
                step(nc.vector.tensor_scalar(keep[:, :, 1:TOP_K], cum[:, :, 0:TOP_K - 1], THRESHOLD, None, ALU.is_lt))
                settle()
                step(nc.vector.tensor_tensor(rw[:], tv[:], keep[:], ALU.mult))
                settle()
                normalised(rw[:], rw[:])
                step(nc.vector.tensor_scalar(active[:, bass.ds(k0, TT), :], rw[:], 0.0, None, ALU.is_gt))
                step(nc.vector.tensor_tensor(prod[:], onehot[:, bass.ds(k0, TT), :, :],
                                             rw[:].unsqueeze(3).to_broadcast([P, TT, TOP_K, E]), ALU.mult))
                settle()
                step(nc.vector.tensor_reduce(eL[:], prod[:].rearrange("p t j e -> p t e j"), AX.X, ALU.add))
                settle()
                step(nc.vector.tensor_scalar(member[:, bass.ds(k0, TT), :], eL[:], 0.0, None, ALU.is_gt))
                dve.wait_ge(comb_stored, 16 * b + 16)
                nc.vector.tensor_scalar(comb[:], eL[:], tg[:, 1:2], None, ALU.mult).then_inc(comb_ready, 1)

            dve.wait_ge(act_consts, 1)
            nc.vector.memset(keep[:], 1.0)
            statistics(front, 0)
            weight_maxima(front, 0)
            mean_over_std(front, 0)
            activation_maxima(front, 0)
            column_ratio(front, 0)
            column_scale(front, 0)
            scale_x(front, 0)
            row_scales(front, 0)
            statistics(front, 1)
            mean_over_std(front, 1)
            weight_maxima(front, 1)
            weight_maxima(back, 0)
            dequantise(front, 0)
            activation_maxima(front, 1)
            column_ratio(front, 1)
            activation_maxima(back, 0)
            column_ratio(back, 0)
            column_scale(back, 0)
            column_scale(front, 1)
            scale_x(back, 0)
            row_scales(back, 0)
            scale_x(front, 1)
            row_scales(front, 1)
            before = count[0]

            def entries(b, last):
                count[:] = [0, before + b * STEPS_PER_PASS]
                dequantise(back, b)
                if not last:
                    statistics(front, b + 2)
                statistics(back, b)
                if not last:
                    mean_over_std(front, b + 2)
                mean_over_std(back, b)
                if not last:
                    dequantise(front, b + 1)
                    activation_maxima(front, b + 2)
                    weight_maxima(front, b + 2)
                    weight_maxima(back, b + 1)
                    column_ratio(front, b + 2)
                else:
                    dequantise(front, b + 1)
                    weight_maxima(back, b + 1)
                activation_maxima(back, b + 1)
                column_ratio(back, b + 1)
                column_scale(back, b + 1)
                if not last:
                    column_scale(front, b + 2)
                choose(b)
                scale_x(back, b + 1)
                row_scales(back, b + 1)
                if not last:
                    scale_x(front, b + 2)
                    row_scales(front, b + 2)
                combine(b)
                assert last or count[0] == STEPS_PER_PASS, count

            with dve.Fori(0, B - 2) as b:
                entries(b, False)
            entries(B - 2, True)
            dequantise(back, B - 1)
            statistics(back, B - 1)
            mean_over_std(back, B - 1)
            choose(B - 1)
            combine(B - 1)

            dve.wait_ge(x2_stored, 16 + 16 * B)
            dve.wait_ge(comb_ready, B)
            dve.wait_ge(ranks_ready, 1)
            step(nc.vector.tensor_copy(tot, pA[1][:].rearrange("p (k e) -> p k e", e=E)))
            settle()
            src, d, flip = tot, 1, 0
            while d < NK:
                dst = pre[flip]
                step(nc.vector.tensor_copy(dst[:, 0:d, :], src[:, 0:d, :]))
                step(nc.vector.tensor_tensor(dst[:, d:NK, :], src[:, d:NK, :], src[:, 0:NK - d, :], ALU.add))
                settle()
                src, d, flip = dst, 2 * d, 1 - flip
            step(nc.vector.tensor_scalar(cnt_i[:], src[:, NK - 1, :], float(P - 1), None, ALU.add))
            settle()
            step(nc.vector.tensor_scalar(tend_i[:], cnt_i[:], 7, None, ALU.logical_shift_right))
            settle()
            step(nc.vector.tensor_scalar(tiles_f[:], tend_i[:], 1.0, None, ALU.max))
            settle()
            step(nc.vector.tensor_tensor_scan(tend[:], one_e[:], tiles_f[:], 0.0, ALU.mult, ALU.add))
            settle()
            step(nc.vector.tensor_copy(tend_i[:], tend[:]))
            step(nc.vector.tensor_scalar(cnt_i[:, 0:1], tend[:, E - 1:E], 1.0, None, ALU.add))
            for g in range(2):
                step(nc.vector.tensor_scalar(cmp[:], tend[:], pidx[:, g:g + 1], None, ALU.is_le))
                settle()
                step(nc.vector.tensor_reduce(eid_c[:, g:g + 1], cmp[:], AX.X, ALU.add))
                settle()
            nc.vector.tensor_scalar(eid_c[:], eid_c[:], float(E - 1), None, ALU.min).then_inc(eid_ready, 1)
            step(nc.vector.tensor_scalar(trips_i[:], cnt_i[:, 0:1], 1, None, ALU.logical_shift_right))
            step(nc.vector.tensor_tensor(base_e[:], tend[:], tiles_f[:], ALU.subtract))
            step(nc.vector.tensor_tensor(slot_e, src[:], tot, ALU.subtract))
            settle()
            step(nc.vector.tensor_tensor(slot_e, slot_e, pA[0][:].rearrange("p (k e) -> p k e", e=E), ALU.add))
            settle()
            step(nc.vector.scalar_tensor_tensor(out=slot_e, in0=base_e[:].unsqueeze(1).to_broadcast([P, NK, E]), scalar=float(P),
                                                in1=slot_e, op0=ALU.mult, op1=ALU.add))
            settle()
            dve.sem_inc(slot_e_ready, 1)
            dve.wait_ge(eidT_ready, 1)
            step(nc.vector.tensor_copy(eid_f[:], pB[0][:, 0:2 * P]))
            step(nc.vector.tensor_copy(eid_i[:], pB[0][:, 0:2 * P]))
            settle()
            settle()
            step(nc.vector.tensor_tensor(tok_f[:, 1:TABW], eid_f[:, 1:TABW], eid_f[:, 0:TABW - 1], ALU.is_gt))
            settle()
            step(nc.vector.scalar_tensor_tensor(out=begin_i[:, 1:TABW], in0=eid_f[:, 1:TABW], scalar=1.0, in1=tok_f[:, 1:TABW],
                                                op0=ALU.add, op1=ALU.mult))
            for b in range(B):
                k = b * TT
                if b % 2 == 0:
                    step(nc.vector.tensor_tensor(choice_slots(b), onehot[:, k:k + TT, :, :],
                                                 slot_e[:, k:k + TT, :].unsqueeze(2).to_broadcast([P, TT, TOP_K, E]), ALU.mult))
                    settle()
                else:
                    dve.wait_ge(products_ready, (b + 1) // 2)
                step(nc.vector.tensor_reduce(slot_f[:, k:k + TT, :], choice_slots(b), AX.X, ALU.add))
            settle()
            step(nc.vector.scalar_tensor_tensor(out=slot_f, in0=active[:], scalar=-32768.0, in1=slot_f,
                                                op0=ALU.mult, op1=ALU.add))
            settle()
            step(nc.vector.tensor_scalar(slot_i, slot_f.rearrange("p k j -> p (k j)"), 32768.0, None, ALU.add))
            settle()
            step(nc.vector.tensor_scalar(lo_i, slot_i, P - 1, None, ALU.bitwise_and))
            step(nc.vector.tensor_scalar(hi_i, slot_i, 7, None, ALU.logical_shift_right))
            settle()
            nc.vector.tensor_copy(lo_f[:], lo_i).then_inc(lo_ready, 1)
            step(nc.vector.tensor_copy(lo_h[:], lo_i))
            step(nc.vector.tensor_copy(hi_h[:], hi_i))
            settle()
            with dve.Fori(0, NK // 2) as it:
                for r in range(2):
                    k = 2 * it + r
                    dve.wait_ge(labelled, k + 1)
                    dve.sem_inc(passed, 1)
                    nc.vector.tensor_tensor(oh_lo[:, r, 0:LO_BY_DVE], iota_lo[:].unsqueeze(1).to_broadcast([P, LO_BY_DVE, P]),
                                            lo_h[:, bass.ds(TOP_K * k, LO_BY_DVE)].unsqueeze(2).to_broadcast([P, LO_BY_DVE, P]),
                                            ALU.is_equal).then_inc(lo_hots, 1)
                    dve.wait_ge(hot_used, k + 1)
                    dve.sem_inc(passed, 1)
                    nc.vector.tensor_tensor(oh_hi[:, r], iota_hi[:].unsqueeze(1).to_broadcast([P, TOP_K, TILES]),
                                            hi_h[:, bass.ds(TOP_K * k, TOP_K)].unsqueeze(2).to_broadcast([P, TOP_K, TILES]),
                                            ALU.is_equal).then_inc(hi_hots, 1)
            dve.wait_ge(tab_ready, 1)
            step(nc.vector.tensor_scalar(pad[:], pB[1][:, 0:TILES], 0.0, pidx[:, 0:1], ALU.is_equal, ALU.mult))
            step(nc.vector.tensor_scalar(tok_f[:, 0:TILES], pB[1][:, 0:TILES], -1.0, float(N), ALU.mult, ALU.add))
            step(nc.vector.tensor_scalar(tok_i[:, TILES:TABW], one_e[:, 0:TABW - TILES], float(N), pidx[:, 0:1], ALU.mult, ALU.add))
            settle()
            nc.vector.tensor_tensor(tok_i[:, 0:TILES], tok_f[:, 0:TILES], pad[:], ALU.add).then_inc(plan_ready, 1)
            dve.wait_ge(plan_ready, 1)
            dve.sem_inc(tok_ready, 1)

            def row_weights(i, q):
                if q == 0:
                    dve.wait_ge(gathered[0], 8 * i + 16)
                else:
                    dve.wait_ge(gathered[1], 8 * i + 8)
                nc.vector.scalar_tensor_tensor(out=pick[q][:], in0=iota_e[:], scalar=eid_f[:, bass.ds(i, 1)], in1=got[q][:, D:ROW],
                                               op0=ALU.is_equal, op1=ALU.mult,
                                               accum_out=wt[:, bass.ds(i, 1)]).then_inc(wt_ready, 1)

            def inner(i, q):
                dve.wait_ge(gs_ready, i + 1)
                nc.vector.tensor_tensor(hh[q][:, 0:F], gs[q], pH[q][:, F:GU], ALU.mult).then_inc(hh_ready, 1)
                nc.vector.tensor_tensor(hh[q][:, F:2 * P], gs[q][:, P:F], pH[q][:, F + P:GU], ALU.mult).then_inc(dup_ready, 1)

            def inner_low(i, q):
                dve.wait_ge(hT_high_ready, i + 1)
                nc.vector.tensor_tensor(hT_low[q][:], pA[q][:, 0:2 * P].rearrange("p (c t) -> p c t", c=2), hT_high[q][:].bitcast(F32),
                                        ALU.subtract).then_inc(hT_low_ready, 1)

            def begins(i):
                return nc.vector.value_load(begin_i[0:1, bass.ds(i, 1)], min_val=0, max_val=E)

            def low_parts(e, number):
                dve.wait_ge(high_ready, number)
                dve.sem_inc(passed, 1)
                nc.vector.tensor_tensor(d_low[:, bass.ds(e % RING, 1)], wd[:, bass.ds(e % RING, 1), 0, :],
                                        d_high[:, bass.ds(e % RING, 1), 0, :].bitcast(F32), ALU.subtract).then_inc(low_ready, 1)
                under = d_high[FREST:P, bass.ds(e % RING, 1), 1, :]
                nc.vector.tensor_tensor(under, wd[FREST:P, bass.ds(e % RING, 1), 1, :], under.bitcast(F32),
                                        ALU.subtract).then_inc(low_ready, 1)

            trips = nc.vector.value_load(trips_i[0:1, 0:1], min_val=1, max_val=TILES // 2)
            low_parts(0, 1)
            row_weights(0, 0)
            row_weights(1, 1)
            inner(0, 0)
            with dve.Fori(0, trips) as it:
                for i, q in ((2 * it + 1, 1), (2 * it + 2, 0)):
                    row_weights(i + 1, 1 - q)
                    inner_low(i - 1, 1 - q)
                    begin = begins(i)
                    with dve.If(begin != 0):
                        low_parts(begin - 1, begin)
                    inner(i, q)


_INS = ["x", "fside_BxS2xS2_0", "ctx_1024", "g_xattn", "g_ffn", "L0_ffn_gate_weight", "L0_ffn_gate_up_proj",
        "L0_ffn_down_proj"]


def kernel(**inputs):
    import numpy as _np
    import concourse.bacc as _bacc
    from concourse import mybir as _mybir
    from concourse.bass_utils import run_bass_kernel_spmd as _run

    data = {n: _np.asarray(inputs[n]) for n in _INS}
    B, T, D = data["x"].shape
    for n in ("g_xattn", "g_ffn"):
        data[n] = _np.broadcast_to(data[n].reshape(1, 1), (P, 1))
    data["L0_ffn_gate_weight"] = data["L0_ffn_gate_weight"].T
    data["L0_ffn_gate_up_proj"] = data["L0_ffn_gate_up_proj"].transpose(0, 2, 1)
    data["L0_ffn_down_proj"] = data["L0_ffn_down_proj"].transpose(0, 2, 1)

    nc = _bacc.Bacc("TRN2", target_bir_lowering=False, num_devices=1)
    arrays, args = {}, []
    for name in _INS:
        a = _np.ascontiguousarray(data[name])
        arrays[f"in_{name}"] = a
        args.append(nc.dram_tensor(f"in_{name}", a.shape, _mybir.dt.from_np(a.dtype), kind="ExternalInput").ap())
    args.append(nc.dram_tensor("out_rows", (B * T + P, D), _mybir.dt.from_np(_np.dtype("float32")), kind="ExternalOutput").ap())
    build(nc, *args)
    r = _run(nc, [arrays], core_ids=[0])
    return r.results[0]["out_rows"][0:B * T].reshape(B, T, D)
```
